# Optimizing a Trainium2 kernel written in Bass

```python
import numpy as np
import jax
import jax.numpy as jnp

def _softmax(x, axis=-1):
    return jax.nn.softmax(x, axis=axis)

def _gelu(x):
    return jax.nn.gelu(x, approximate=True)

def _silu(x):
    return jax.nn.silu(x)

def _sigmoid(x):
    return jax.nn.sigmoid(x)

def _layernorm(x, axis=-1, eps=1e-05):
    m = jnp.mean(x, axis=axis, keepdims=True)
    v = jnp.var(x, axis=axis, keepdims=True)
    return (x - m) / jnp.sqrt(v + eps)

def _scatter_add(tgt, idx, src, axis=0):
    return tgt.at[idx].add(src)

def _segment_sum(src, seg, n):
    return jax.ops.segment_sum(src, seg, n)
kernel_name = 'mk_xattn_seq_d2_seqx_r4_9d0eec'

def setup_inputs(seed: int=0):
    np.random.seed(seed)
    _w = jnp.asarray

    def _rec_inputs():
        import jax
        import jax.numpy as jnp
        _rk = jax.random.key(seed)
        x = -0.000125 + 0.9999 * jax.random.normal(jax.random.fold_in(_rk, 1), (8, 512, 256), jnp.float32)
        _lenS = 512 - jax.random.randint(jax.random.fold_in(_rk, 7), (8,), 0, max(1, 512 // 4) + 1, jnp.int32)
        _lenS2 = 1601 - jax.random.randint(jax.random.fold_in(_rk, 8), (8,), 0, max(1, 1601 // 4) + 1, jnp.int32)
        _ctx_512P = jax.random.normal(jax.random.fold_in(_rk, 11), (8, 16, 128), jnp.float32)
        _ctx_512c = jax.random.dirichlet(jax.random.fold_in(_rk, 511), 0.3 * jnp.ones((16,), jnp.float32), (8, 1601))
        _ctx_512t = jnp.einsum('bsk,bkd->bsd', _ctx_512c, _ctx_512P)
        _ctx_512t = _ctx_512t * jax.lax.rsqrt(jnp.mean(jnp.square(_ctx_512t)) + 1e-12) * 0.953939
        ctx_512 = 0.000227908 + 0.99994 * (_ctx_512t + 0.3 * jax.random.normal(jax.random.fold_in(_rk, 611), (8, 1601, 128), jnp.float32))
        return (x, ctx_512)
    x, ctx_512 = _rec_inputs()

    def _L0_xattn_setup():
        import jax, jax.numpy as jnp
        import numpy as np
        B, T, E = (8, 1024, 256)
        M, L = (64, 128)
        EPS = 1e-06
        key = jax.random.key(seed)
        ks = jax.random.split(key, 5)
        return {'emb': jax.random.normal(ks[0], (B, T, E), dtype=jnp.float32), 'latent': jax.random.normal(ks[1], (B, M, L), dtype=jnp.float32), 'Wq': jax.random.normal(ks[2], (E, E), dtype=jnp.float32) * (1.0 / np.sqrt(E)), 'bq': jnp.zeros((E,), dtype=jnp.float32), 'Wk': jax.random.normal(ks[3], (L, E), dtype=jnp.float32) * (1.0 / np.sqrt(L)), 'bk': jnp.zeros((E,), dtype=jnp.float32), 'Wv': jax.random.normal(ks[4], (L, E), dtype=jnp.float32) * (1.0 / np.sqrt(L)), 'bv': jnp.zeros((E,), dtype=jnp.float32), 'gamma': jnp.ones((E,), dtype=jnp.float32), 'beta': jnp.zeros((E,), dtype=jnp.float32)}
    _L0_xattn_all = _L0_xattn_setup()
    _L0_xattn_in = {k: v for k, v in _L0_xattn_all.items() if k in ('Wq', 'bq', 'Wk', 'bk', 'Wv', 'bv', 'gamma', 'beta')}
    del _L0_xattn_all

    def _L1_xattn_setup():
        import jax, jax.numpy as jnp
        import numpy as np
        QUERY_DIM = 256
        KEY_DIM = 128
        HIDDEN_DIM = 256
        B, LQ, LK = (8, 512, 512)
        key = jax.random.key(seed)
        ks = jax.random.split(key, 10)
        s_q = 1.0 / np.sqrt(QUERY_DIM)
        s_k = 1.0 / np.sqrt(KEY_DIM)
        s_h = 1.0 / np.sqrt(HIDDEN_DIM)
        return {'query': jax.random.normal(ks[0], (B, LQ, QUERY_DIM), jnp.float32), 'key': jax.random.normal(ks[1], (B, LK, KEY_DIM), jnp.float32), 'Wq': jax.random.uniform(ks[2], (QUERY_DIM, HIDDEN_DIM), jnp.float32, -s_q, s_q), 'bq': jax.random.uniform(ks[3], (HIDDEN_DIM,), jnp.float32, -s_q, s_q), 'Wk': jax.random.uniform(ks[4], (KEY_DIM, HIDDEN_DIM), jnp.float32, -s_k, s_k), 'bk': jax.random.uniform(ks[5], (HIDDEN_DIM,), jnp.float32, -s_k, s_k), 'Wv': jax.random.uniform(ks[6], (KEY_DIM, HIDDEN_DIM), jnp.float32, -s_k, s_k), 'bv': jax.random.uniform(ks[7], (HIDDEN_DIM,), jnp.float32, -s_k, s_k), 'Wo': jax.random.uniform(ks[8], (HIDDEN_DIM, QUERY_DIM), jnp.float32, -s_h, s_h), 'bo': jax.random.uniform(ks[9], (QUERY_DIM,), jnp.float32, -s_h, s_h)}
    _L1_xattn_all = _L1_xattn_setup()
    _L1_xattn_in = {k: v for k, v in _L1_xattn_all.items() if k in ('Wq', 'bq', 'Wk', 'bk', 'Wv', 'bv', 'Wo', 'bo')}
    del _L1_xattn_all
    return {'x': x, 'ctx_512': ctx_512, 'L0_xattn_Wq': _L0_xattn_in['Wq'], 'L0_xattn_bq': _L0_xattn_in['bq'], 'L0_xattn_Wk': _L0_xattn_in['Wk'], 'L0_xattn_bk': _L0_xattn_in['bk'], 'L0_xattn_Wv': _L0_xattn_in['Wv'], 'L0_xattn_bv': _L0_xattn_in['bv'], 'L0_xattn_gamma': _L0_xattn_in['gamma'], 'L0_xattn_beta': _L0_xattn_in['beta'], 'L1_xattn_Wq': _L1_xattn_in['Wq'], 'L1_xattn_bq': _L1_xattn_in['bq'], 'L1_xattn_Wk': _L1_xattn_in['Wk'], 'L1_xattn_bk': _L1_xattn_in['bk'], 'L1_xattn_Wv': _L1_xattn_in['Wv'], 'L1_xattn_bv': _L1_xattn_in['bv'], 'L1_xattn_Wo': _L1_xattn_in['Wo'], 'L1_xattn_bo': _L1_xattn_in['bo']}

def reference(x, ctx_512, L0_xattn_Wq, L0_xattn_bq, L0_xattn_Wk, L0_xattn_bk, L0_xattn_Wv, L0_xattn_bv, L0_xattn_gamma, L0_xattn_beta, L1_xattn_Wq, L1_xattn_bq, L1_xattn_Wk, L1_xattn_bk, L1_xattn_Wv, L1_xattn_bv, L1_xattn_Wo, L1_xattn_bo):
    import jax
    import jax.numpy as jnp

    def _L0_xattn_ref(emb, latent, Wq, bq, Wk, bk, Wv, bv, gamma, beta):
        import jax, jax.numpy as jnp
        import numpy as np
        B, T, E = (8, 1024, 256)
        M, L = (64, 128)
        EPS = 1e-06
        q = jnp.einsum('bte,ef->btf', emb, Wq) + bq
        k = jnp.einsum('bml,le->bme', latent, Wk) + bk
        v = jnp.einsum('bml,le->bme', latent, Wv) + bv
        scale = 1.0 / jnp.sqrt(jnp.asarray(E, dtype=q.dtype))
        w = jnp.einsum('bte,bme->btm', q, k) * scale
        w = jax.nn.softmax(w, axis=1)
        pred = jnp.einsum('btm,bme->bte', w, v)
        x = pred + emb
        mu = jnp.mean(x, axis=-1, keepdims=True)
        var = jnp.var(x, axis=-1, keepdims=True)
        return (x - mu) * jax.lax.rsqrt(var + EPS) * gamma + beta

    def _L1_xattn_ref(query, key, Wq, bq, Wk, bk, Wv, bv, Wo, bo):
        import jax, jax.numpy as jnp
        import numpy as np
        QUERY_DIM = 256
        KEY_DIM = 128
        HIDDEN_DIM = 256
        B, LQ, LK = (8, 512, 512)
        scale = HIDDEN_DIM ** (-0.5)
        Q = jnp.einsum('bqd,dh->bqh', query, Wq) + bq
        K = jnp.einsum('bkd,dh->bkh', key, Wk) + bk
        V = jnp.einsum('bkd,dh->bkh', key, Wv) + bv
        scores = jnp.einsum('bqh,bkh->bqk', Q, K) * scale
        weights = jax.nn.softmax(scores, axis=-1)
        attended = jnp.einsum('bqk,bkh->bqh', weights, V)
        out = jnp.einsum('bqh,hd->bqd', attended, Wo) + bo
        return query + out
    x = _L0_xattn_ref(x, ctx_512, L0_xattn_Wq, L0_xattn_bq, L0_xattn_Wk, L0_xattn_bk, L0_xattn_Wv, L0_xattn_bv, L0_xattn_gamma, L0_xattn_beta)
    x = _L1_xattn_ref(x, ctx_512, L1_xattn_Wq, L1_xattn_bq, L1_xattn_Wk, L1_xattn_bk, L1_xattn_Wv, L1_xattn_bv, L1_xattn_Wo, L1_xattn_bo)
    return x

_drawn_inputs = setup_inputs


def setup_inputs(seed=0):
    import zlib

    import numpy as np

    out = dict(_drawn_inputs(seed))
    spreads = {'L0_xattn_bq': (0.0, 0.8),
     'L0_xattn_bk': (0.0, 0.1),
     'L0_xattn_bv': (0.0, 0.1),
     'L0_xattn_gamma': (1.0, 0.2),
     'L0_xattn_beta': (0.0, 0.1)}
    factors = {'L1_xattn_Wq': 2.681, 'L1_xattn_bq': 8.0, 'L1_xattn_Wk': 2.685, 'L1_xattn_bk': 8.0}
    for name, (base, spread) in spreads.items():
        noise = np.random.default_rng([zlib.crc32(name.encode()), seed]).standard_normal(out[name].shape)
        drawn = base * np.exp(spread * noise) if base else spread * noise
        out[name] = jnp.asarray(drawn.astype(out[name].dtype))
    for name, factor in factors.items():
        out[name] = (out[name] * factor).astype(out[name].dtype)
    return out
```

```python
from collections import namedtuple
from contextlib import ExitStack

import concourse.bass as bass
from concourse import mybir

ALU = mybir.AluOpType
ACT = mybir.ActivationFunctionType
F32 = mybir.dt.float32
F32R = mybir.dt.float32r
AX_X = mybir.AxisListType.X

P = 128
BANK = 512
LN_EPS = 1e-6
BIG = 3.0e38

TENSOR_ORDER = (
    ("scores0", "a", 7), ("turn_ctx", "a", 2), ("weigh0", "a", 3), ("scores1", "b", 0), ("scores1", "b", 1),
    ("scores1", "b", 2), ("scores1", "b", 3), ("scores0", "a", 8), ("turn_x", "c", 0), ("weigh0", "a", 4),
    ("weigh0", "a", 5), ("scores1", "b", 4), ("scores1", "b", 5), ("scores1", "b", 6), ("scores1", "b", 7),
    ("turn_x", "c", 1), ("scores0", "a", 9), ("scores1", "b", 8), ("scores1", "b", 9), ("scores1", "b", 10),
    ("scores1", "b", 11), ("project_q0", "c", 0), ("weigh0", "a", 6), ("scores1", "b", 12), ("scores1", "b", 13),
    ("scores1", "b", 14), ("scores1", "b", 15), ("weigh0", "a", 7), ("scores0", "a", 10), ("scores0", "a", 11),
    ("weigh0", "a", 8), ("turn_p1", "b", 0), ("turn_ctx", "a", 3), ("turn_p1", "b", 1), ("weigh0", "a", 9),
    ("turn_ctx", "c", 0), ("scores0", "a", 12), ("turn_p1", "b", 2), ("weigh1", "b", 0), ("weigh1", "b", 1),
    ("turn_p1", "b", 3), ("project_bias0", "c", 0), ("weigh0", "a", 10), ("turn_p1", "b", 4), ("scores0", "c", 0),
    ("turn_p1", "b", 5), ("weigh1", "b", 2), ("scores0", "c", 1), ("turn_p1", "b", 6), ("weigh1", "b", 3),
    ("weigh0", "a", 11), ("turn_ctx", "c", 1), ("scores0", "c", 2), ("turn_p1", "b", 7), ("weigh1", "b", 4),
    ("weigh0", "a", 12), ("scores0", "c", 3), ("weigh1", "b", 5), ("turn_p1", "b", 8), ("turn_p1", "b", 9),
    ("weigh1", "b", 6), ("weigh1", "b", 7), ("predict", "a", 0), ("weigh0", "c", 0), ("turn_p1", "b", 10),
    ("turn_p1", "b", 11), ("scores0", "c", 4), ("predict", "a", 1), ("weigh0", "c", 1), ("weigh1", "b", 8),
    ("weigh1", "b", 9), ("turn_p1", "b", 12), ("weigh1", "b", 10), ("weigh1", "b", 11), ("scores0", "c", 5),
    ("weigh1", "b", 12), ("weigh0", "c", 2), ("project_out", "b", 0), ("project_out", "b", 1), ("turn_y", "a", 0),
    ("turn_y", "a", 1), ("scores0", "c", 6), ("project_q1", "a", 0),
)
SCALAR_ORDER = (
    ("exp0", "a", 6), ("p0_high", "a", 6), ("exp1", "b", 0), ("exp0", "a", 7), ("exp1", "b", 1), ("x_turned", "c", 0),
    ("p0_high", "a", 7), ("x_turned", "c", 1), ("exp1", "b", 2), ("exp0", "a", 8), ("exp1", "b", 3),
    ("p0_high", "a", 8), ("exp0", "a", 9), ("ctx_split", "a", 3), ("exp1", "b", 4), ("exp1", "b", 5),
    ("p0_high", "a", 9), ("q0_high", "c", 0), ("exp1", "b", 6), ("exp1", "b", 7), ("exp0", "a", 10),
    ("ctx_high", "a", 3), ("p0_high", "a", 10), ("p1_turned", "b", 0), ("p1_turned", "b", 1), ("exp0", "a", 11),
    ("ctx_high", "c", 0), ("p1_turned", "b", 2), ("p0_high", "a", 11), ("exp0", "a", 12), ("bias0", "c", 0),
    ("p1_turned", "b", 3), ("p0_high", "a", 12), ("p1_turned", "b", 4), ("p1_turned", "b", 5), ("ctx_split", "c", 0),
    ("p1_turned", "b", 6), ("exp0", "c", 0), ("p1_turned", "b", 7), ("ctx_high", "c", 1), ("exp0", "c", 1),
    ("p0_high", "c", 0), ("weighed0", "a", 0), ("p1_turned", "b", 8), ("p0_high", "c", 1), ("p1_turned", "b", 9),
    ("exp0", "c", 2), ("p1_turned", "b", 10), ("p1_turned", "b", 11), ("p0_high", "c", 2), ("exp0", "c", 3),
    ("p0_high", "c", 3), ("exp0", "c", 4), ("p1_turned", "b", 12), ("weighed1", "b", 0), ("exp0", "c", 5),
    ("p0_high", "c", 4), ("y_turned", "a", 0), ("y_turned", "a", 1), ("p0_high", "c", 5), ("q1_high", "a", 0),
    ("ctx_split", "c", 1), ("ctx_high", "c", 2), ("ctx_split", "c", 2),
)
VECTOR_ORDER = (
    ("p0_low", "a", 5), ("ctx_low", "a", 2), ("rowmax1", "b", 0), ("rowmax1", "b", 1), ("recip0", "a", 6),
    ("rowmax1", "b", 2), ("rowmax1", "b", 3), ("bias1_of", "b", 0), ("p0_low", "a", 6), ("max0", "a", 7),
    ("recip0", "a", 7), ("rowmax1", "b", 4), ("rowmax1", "b", 5), ("rowmax1", "b", 6), ("rowmax1", "b", 7),
    ("bias1_of", "b", 1), ("max0", "a", 8), ("p0_low", "a", 7), ("max0", "a", 9), ("recip0", "a", 8),
    ("rowmax1", "b", 8), ("rowmax1", "b", 9), ("rowmax1", "b", 10), ("rowmax1", "b", 11), ("bias1_of", "b", 2),
    ("recip0", "a", 9), ("p0_low", "a", 8), ("rowmax1", "b", 12), ("rowmax1", "b", 13), ("rowmax1", "b", 14),
    ("rowmax1", "b", 15), ("bias1_of", "b", 3), ("q0_low", "c", 0), ("max0", "a", 10), ("p0_low", "a", 9),
    ("recip1", "b", 0), ("recip0", "a", 10), ("ctx_low", "a", 3), ("max0", "a", 11), ("p0_low", "a", 10),
    ("p1_low", "b", 0), ("p1_low", "b", 1), ("recip0", "a", 11), ("ctx_low", "c", 0), ("max0", "a", 12),
    ("p0_low", "a", 11), ("p1_low", "b", 2), ("recip0", "a", 12), ("p1_low", "b", 3), ("p1_low", "b", 4),
    ("p0_low", "a", 12), ("p1_low", "b", 5), ("max0", "c", 0), ("p1_low", "b", 6), ("max0", "c", 1),
    ("p1_low", "b", 7), ("recip0", "c", 0), ("ctx_low", "c", 1), ("p0_low", "c", 0), ("recip0", "c", 1),
    ("max0", "c", 2), ("p1_low", "b", 8), ("p1_low", "b", 9), ("recip0", "c", 2), ("p0_low", "c", 1),
    ("max0", "c", 3), ("residual0", "a", 0), ("moments0", "a", 0), ("p1_low", "b", 10), ("p1_low", "b", 11),
    ("recip0", "c", 3), ("p0_low", "c", 2), ("residual0", "a", 1), ("max0", "c", 4), ("p0_low", "c", 3),
    ("p1_low", "b", 12), ("moments0", "a", 1), ("max0", "c", 5), ("recip0", "c", 4), ("normalised", "a", 0),
    ("normalised", "a", 1), ("finish", "b", 0), ("recip0", "c", 5), ("finish", "b", 1), ("bias_row1", "a", 0),
    ("max0", "c", 6), ("p0_low", "c", 4), ("q1_low", "a", 0),
)
GPSIMD_ORDER = (
    ("sum_weights", "a", 4), ("sum_weights", "a", 5), ("residual1", "b", 0), ("ctx_low", "a", 2),
    ("sum_weights", "a", 6), ("sum_weights", "a", 7), ("sum_weights", "a", 8), ("sum_weights", "a", 9),
    ("sum_weights", "a", 10), ("sum_weights", "a", 11), ("ctx_low", "a", 3), ("sum_weights", "a", 12),
    ("ctx_low", "c", 0), ("sum_weights", "c", 0), ("sum_weights", "c", 1), ("rsqrt_var", "a", 0),
    ("sum_weights", "c", 2), ("rsqrt_var", "a", 1), ("sum_weights", "c", 3), ("ctx_low", "c", 1),
)

Batch = namedtuple("Batch", "n use par")


def batch(pair, k):
    return Batch(2 * pair + k, pair + k // 2, k % 2)


def first(bt):
    return isinstance(bt.n, int) and bt.n == 0


def xattn_kernel(nc, x, ctx, wq0, bq0, wk0, bk0, wv0, bv0, gamma, beta,
                 wq1, bq1, wk1, bk1, wv1, bv1, wo, bo, out):
    B, T, E = x.shape
    _, M, L = ctx.shape
    TB = T // P
    EC = E // P
    MT = -(-M // P)
    MPAD = M + M % 2
    GROUPS = -(-MT // TB)
    SCALE = float(E) ** -0.5
    RING = 4

    def ring0(i):
        return 4 if i == MT - 1 else i % 4

    def before0(a, i):
        last = i - 4 if 4 <= i < MT - 1 else (i + 8 - MT if i < 4 else -1)
        if last < 0 and isinstance(a.n, int) and a.n == 0:
            return None
        return MT * a.n + last + 1

    PAIRS = (B - 2) // 2
    assert L == P and T == BANK and EC == 2 and TB == 4 and B % 2 == 0

    def rows(i):
        return min(P, M - i * P)

    def group(g):
        return range(TB * g, min(TB * g + TB, MT))

    def group_cols(g):
        return TB * g * P, min(M, TB * (g + 1) * P)

    halves = (slice(0, 2 * BANK), slice(2 * BANK, M))
    chunks = [(c, min(MPAD, c + BANK)) for c in range(0, MPAD, BANK)]

    with ExitStack() as stack:
        def sb(name, shape, dt=F32):
            return stack.enter_context(nc.sbuf_tensor(name, shape, dt))

        def sem(name):
            return stack.enter_context(nc.semaphore(name))

        p1 = sb("p1", [P, TB, M])
        p1_flat = p1[:].rearrange("p t m -> p (t m)")
        room = [0]

        def early(n):
            room[0] += n
            return p1_flat[:, room[0] - n:room[0]]

        ident = sb("ident", [P, P])
        ones = sb("ones", [P, P])
        wq_sb = [early(EC * E).rearrange("p (c h) -> p c h", c=EC) for _ in range(2)]
        wk_sb = [early(E) for _ in range(2)]
        wv0_sb = sb("wv0_sb", [P, E])
        wv1_sb = early(E)
        wo_sb = early(EC * E).rearrange("p (c d) -> p c d", c=EC)
        NV = 7
        vec_rows = sb("vec_rows", [NV, E])
        cols = sb("cols", [P, EC, NV])
        bq_col = [cols[:, :, 0], cols[:, :, 2]]
        bk_col = [cols[:, :, 1], cols[:, :, 3]]
        bv1_col, gamma_col, beta_col = cols[:, :, 4], cols[:, :, 5], cols[:, :, 6]
        bv0_row = sb("bv0_row", [P, E])
        gamma_row = sb("gamma_row", [P, E])
        beta_row = sb("beta_row", [P, E])
        bo_row = sb("bo_row", [P, E])
        wqT = [early(EC * E).rearrange("p (h e) -> p h e", h=EC) for _ in range(2)]
        wkT = early(2 * EC * P).rearrange("p (n h l) -> p n h l", n=2, h=EC)
        wvT = early(EC * P).rearrange("p (h l) -> p h l", h=EC)
        bk_rep = [early(EC * P).rearrange("p (h l) -> p h l", h=EC) for _ in range(2)]
        bv1_rep = early(EC * P).rearrange("p (h l) -> p h l", h=EC)
        a_sb = sb("a_sb", [P, 2, EC, P])
        a1_gamma = sb("a1_gamma", [P, EC, P])
        u0_rep = sb("u0_rep", [P, EC, P])
        u1_row = sb("u1_row", [P, E])
        u1_gamma = sb("u1_gamma", [P, E])
        w2_sb = sb("w2_sb", [P, E])
        betaob_row = sb("betaob_row", [P, E])
        betaob_part = sb("betaob_part", [P, E])
        small = sb("small", [P, 4])
        qb0 = small[:, 0:1]
        bqbk0 = small[:, 2:3]
        MADE = 7
        scaled1 = sb("scaled1", [P, 2])
        c1_const = sb("c1_const", [P, 1])
        junk = sb("junk", [P, TB, E])

        x_sb = [sb(f"x_sb{p}", [P, TB, E]) for p in range(2)]
        ctx_sb = sb("ctx_sb", [P, MT, L])
        ctx_hi = [sb(f"ctx_hi{p}", [P, MT, L], F32R) for p in range(2)]
        ctx_lo = [sb(f"ctx_lo{p}", [P, MT, L], F32R) for p in range(2)]
        ctxT_hi = [sb(f"ctxT_hi{p}", [P, MPAD], F32R) for p in range(2)]
        ctxT_lo = [sb(f"ctxT_lo{p}", [P, MPAD], F32R) for p in range(2)]
        xT = sb("xT", [P, EC, T])
        qw0_hi = [sb(f"qw0_hi{p}", [P, T], F32R) for p in range(2)]
        qw0_lo = [sb(f"qw0_lo{p}", [P, T], F32R) for p in range(2)]
        cb = [sb(f"cb{p}", [P, T]) for p in range(2)]
        s0_sb = sb("s0_sb", [P, 2, T])
        min0 = sb("min0", [P, MT])
        sum0 = sb("sum0", [P, MT])
        r0 = sb("r0", [P, MT])
        p0 = sb("p0", [P, 5, T])
        p0_hi = sb("p0_hi", [P, 5, T], F32R)
        p0_lo = sb("p0_lo", [P, 5, T], F32R)
        wsum = [sb(f"wsum{p}", [P, T]) for p in range(2)]
        at0 = sb("at0", [P, T])
        xr = sb("xr", [P, TB, E])
        stats = sb("stats", [P, TB, 6])
        mv = sb("mv", [P, TB, 2])
        var_eps = sb("var_eps", [P, TB, 1])
        rstd = sb("rstd", [P, TB, 1])
        neg_half = sb("neg_half", [P, 2, 1])
        xhat = sb("xhat", [P, TB, E])
        y_res = sb("y_res", [P, TB, E])
        xhT = xT
        qw1_hi = sb("qw1_hi", [P, T], F32R)
        qw1_lo = sb("qw1_lo", [P, T], F32R)
        c1 = sb("c1", [P, TB])
        max1 = sb("max1", [P, TB, len(chunks)])
        neg_max1 = sb("neg_max1", [P, TB])
        bias1 = sb("bias1", [P, TB])
        sum1 = sb("sum1", [P, 2, TB])
        sum1_all = sb("sum1_all", [P, TB])
        r1 = sb("r1", [P, TB])
        p1T_hi = sb("p1T_hi", [P, RING, T], F32R)
        p1T_lo = sb("p1T_lo", [P, RING, T], F32R)
        at1 = sb("at1", [P, T])
        o_sb = sb("o_sb", [P, TB, E])

        ps_s0 = stack.enter_context(nc.psum_tensor("ps_s0", [P, 2, BANK], F32))
        ps_acc0 = stack.enter_context(nc.psum_tensor("ps_acc0", [P, BANK], F32))
        ps_s1 = stack.enter_context(nc.psum_tensor("ps_s1", [P, 4 * BANK], F32))
        ps_misc = stack.enter_context(nc.psum_tensor("ps_misc", [P, BANK], F32))

        def s1_bank(k):
            return ps_s1[:, k * BANK:(k + 1) * BANK]

        ps_turn = [s1_bank(k) for k in range(3)]
        ps_y = [s1_bank(0), s1_bank(3)]
        ps_q1 = s1_bank(0)
        ps_out = [s1_bank(1), s1_bank(2)]
        ps_acc1 = s1_bank(3)

        ident_zero, ident_done, ones_done = sem("ident_zero"), sem("ident_done"), sem("ones_done")
        pad_done = sem("pad_done")
        w_loaded, wv_loaded, cols_loaded = sem("w_loaded"), sem("wv_loaded"), sem("cols_loaded")
        rows_loaded = sem("rows_loaded")
        cols_turned, cols_done = sem("cols_turned"), sem("cols_done")
        wT_turned, wT_copied, reps_done = sem("wT_turned"), sem("wT_copied"), sem("reps_done")
        made_ps, a_copied, made_sb = sem("made_ps"), sem("a_copied"), sem("made_sb")
        small_ps, small_sb, beta_dot = sem("small_ps"), sem("small_sb"), sem("beta_dot")
        x_loaded = [sem(f"x_loaded{p}") for p in range(2)]
        ctx_loaded = [sem(f"ctx_loaded{g}") for g in range(GROUPS)]
        out_free = [sem(f"out_free{h}") for h in range(2)]
        ctxT_ps, xT_ps, qw0_ps, cb_ps = sem("ctxT_ps"), sem("xT_ps"), sem("qw0_ps"), sem("cb_ps")
        s0_ps, pv0_ps, pred_ps = sem("s0_ps"), sem("pv0_ps"), sem("pred_ps")
        xhT_ps, qw1_ps, s1_ps, p1T_ps, pv1_ps, out_ps = (
            sem("xhT_ps"), sem("qw1_ps"), sem("s1_ps"), sem("p1T_ps"), sem("pv1_ps"), sem("out_ps"))
        ctxT_hi_done, xT_done, qw0_hi_done, cb_done = (
            sem("ctxT_hi_done"), sem("xT_done"), sem("qw0_hi_done"), sem("cb_done"))
        exp0_done, at0_done = sem("exp0_done"), sem("at0_done")
        xhT_done, qw1_hi_done, exp1_done, at1_done = (
            sem("xhT_done"), sem("qw1_hi_done"), sem("exp1_done"), sem("at1_done"))
        ctx_hi_done, p0_hi_done, p1T_hi_done = sem("ctx_hi_done"), sem("p0_hi_done"), sem("p1T_hi_done")
        ctxT_lo_done, qw0_lo_done, s0_read, r0_done = (
            sem("ctxT_lo_done"), sem("qw0_lo_done"), sem("s0_read"), sem("r0_done"))
        sum1_done = sem("sum1_done")
        p0_lo_done, p1T_lo_done = sem("p0_lo_done"), sem("p1T_lo_done")
        xr_done, stats_done, mv_done, rstd_done, xhat_done = (
            sem("xr_done"), sem("stats_done"), sem("mv_done"), sem("rstd_done"), sem("xhat_done"))
        c1_done, qw1_lo_done, max1_done, neg_max1_done, bias1_done, r1_done, o_done = (
            sem("c1_done"), sem("qw1_lo_done"), sem("max1_done"), sem("neg_max1_done"), sem("bias1_done"),
            sem("r1_done"), sem("o_done"))
        var_done, wsum_part = sem("var_done"), sem("wsum_part")
        ctx_lo_done, wsum_done, y_part_done, y_res_done = (
            sem("ctx_lo_done"), sem("wsum_done"), sem("y_part_done"), sem("y_res_done"))

        apart_regs = {eng: eng.alloc_register("apart") for eng in (nc.vector, nc.gpsimd)}

        def wait_apart(eng, semaphore, value):
            if not isinstance(value, int):
                apart_reg = apart_regs[eng]
                eng.reg_mov(apart_reg, value)
                value = eng.snap(apart_reg, min_val=1)
            eng.wait_ge(ident_done, 1)
            eng.wait_ge(semaphore, value)

        blk = stack.enter_context(nc.Block())

        def run(body, pre, eng):
            pre()
            body(None, None, batch(0, 0))
            body(batch(0, 0), None, batch(0, 1))
            with eng.Fori(0, PAIRS) as pair:
                body(batch(pair, 1), batch(pair, 0), batch(pair, 2))
                body(batch(pair, 2), batch(pair, 1), batch(pair, 3))
            body(batch(PAIRS, 1), batch(PAIRS, 0), None)
            body(None, batch(PAIRS, 1), None)

        @blk.sync
        def _(sp):
            def load_x(c, after=None):
                if after is not None:
                    sp.wait_ge(xr_done, 2 * (c.n - 1))
                sp.dma_start(x_sb[c.par][:], x[bass.ds(c.n, 1)].rearrange("o (t p) e -> p (o t) e", p=P)
                             ).then_inc(x_loaded[c.par], 16)

            def load_ctx(c, g, after=None):
                if after is not None:
                    sp.wait_ge(ctxT_ps, GROUPS * (c.n - 1) + g + 1)
                    sp.wait_ge(ctx_lo_done, GROUPS * (c.n - 1) + g + 1)
                full = [i for i in group(g) if rows(i) == P]
                dst = ctx_sb
                if full:
                    src = ctx[bass.ds(c.n, 1), full[0] * P:(full[-1] + 1) * P, :]
                    sp.dma_start(dst[:, full[0]:full[-1] + 1, :], src.rearrange("o (i p) l -> p (o i) l", p=P)
                                 ).then_inc(ctx_loaded[g], 16)
                else:
                    i = group(g)[0]
                    src = ctx[bass.ds(c.n, 1), i * P:M, :]
                    sp.dma_start(dst[0:rows(i), i, :], src.rearrange("o p l -> (o p) l")
                                 ).then_inc(ctx_loaded[g], 16)

            def pre():
                for n, w in enumerate((wq0, wq1)):
                    sp.dma_start(wq_sb[n], w.rearrange("(c p) h -> p c h", p=P)).then_inc(w_loaded, 16)
                for n, w in enumerate((wk0, wk1)):
                    sp.dma_start(wk_sb[n], w).then_inc(w_loaded, 16)
                load_x(batch(0, 0))
                for g in range(GROUPS):
                    load_ctx(batch(0, 0), g)
                load_x(batch(0, 1))

            def body(a, b, c):
                if b and c:
                    load_x(c, after=True)
                if a and c:
                    for g in range(GROUPS):
                        load_ctx(c, g, after=True)
                if b is None:
                    return
                dst = out[bass.ds(b.n, 1)].rearrange("o (t p) e -> p (o t) e", p=P)
                for h in range(2):
                    sp.wait_ge(o_done, 2 * b.n + h + 1)
                    sp.dma_start(dst[:, 2 * h:2 * h + 2, :], o_sb[:, 2 * h:2 * h + 2, :]
                                 ).then_inc(out_free[h], 16)

            run(body, pre, sp)
            for h in range(2):
                sp.wait_ge(out_free[h], 16 * (B + 1))

        @blk.tensor
        def _(pe):
            def split3(ps, w_hi, w_lo, m_hi, m_lo, start=True, stop=True):
                nc.tensor.matmul(ps, w_lo, m_hi, start=start, stop=False)
                nc.tensor.matmul(ps, w_hi, m_lo, start=False, stop=False)
                return nc.tensor.matmul(ps, w_hi, m_hi, start=False, stop=stop)

            def turn_ctx(a, g):
                pe.wait_ge(ctx_loaded[g], 16 * (a.n + 1))
                for k, i in enumerate(group(g)):
                    m = rows(i)
                    mm = nc.tensor.transpose(ps_misc[:, k * P:k * P + m], ctx_sb[0:m, i, :],
                                             ident[0:m, 0:m])
                mm.then_inc(ctxT_ps, 1)

            def turn_x(a, c):
                if c == 0:
                    pe.wait_ge(x_loaded[a.par], 16 * (a.use + 1))
                for t in range(TB):
                    mm = nc.tensor.transpose(ps_misc[:, t * P:(t + 1) * P], x_sb[a.par][:, t, c * P:(c + 1) * P],
                                             ident[:])
                mm.then_inc(xT_ps, 1)

            def project_q0(a, _):
                pe.wait_ge(xT_done, EC * (a.n + 1))
                for c in range(EC):
                    mm = nc.tensor.matmul(ps_misc[:], a_sb[:, 0, c, :], xT[:, c, :], start=(c == 0), stop=(c == EC - 1))
                mm.then_inc(qw0_ps, 1)

            def project_bias0(a, _):
                for c in range(EC):
                    mm = nc.tensor.matmul(ps_misc[:], u0_rep[:, c, :], xT[:, c, :], start=(c == 0), stop=(c == EC - 1))
                mm.then_inc(cb_ps, 1)

            def scores0(a, i):
                if i % TB == 0:
                    pe.wait_ge(ctxT_lo_done, GROUPS * a.n + i // TB + 1)
                if i == 0:
                    pe.wait_ge(qw0_lo_done, a.n + 1)
                if i >= 2 or not first(a):
                    pe.wait_ge(s0_read, MT * a.n + i - 1)
                m = slice(i * P, i * P + rows(i))
                split3(ps_s0[0:rows(i), (a.par + i) % 2, :], ctxT_hi[a.par][:, m], ctxT_lo[a.par][:, m],
                       qw0_hi[a.par][:], qw0_lo[a.par][:]).then_inc(s0_ps, 1)

            def weigh0(a, i):
                pe.wait_ge(p0_lo_done, MT * a.n + i + 1)
                if i % TB == 0:
                    pe.wait_ge(ctx_lo_done, GROUPS * a.n + i // TB + 1)
                if i == 0 and not first(a):
                    pe.wait_ge(at0_done, a.n)
                m = rows(i)
                split3(ps_acc0[:], ctx_hi[a.par][0:m, i, :], ctx_lo[a.par][0:m, i, :], p0_hi[0:m, ring0(i), :],
                       p0_lo[0:m, ring0(i), :], start=(i == 0), stop=(i == MT - 1)).then_inc(pv0_ps, 1)

            def predict(a, h):
                if h == 0:
                    pe.wait_ge(at0_done, a.n + 1)
                    pe.wait_ge(wsum_done, MT * (a.n + 1))
                for k in range(2):
                    t = slice((2 * h + k) * P, (2 * h + k + 1) * P)
                    o = ps_misc[:, k * E:(k + 1) * E]
                    nc.tensor.matmul(o, at0[:, t], wv0_sb[:], start=True, stop=False)
                    mm = nc.tensor.matmul(o, wsum[a.par][:, t], bv0_row[:], start=False, stop=True)
                mm.then_inc(pred_ps, 1)

            def turn_y(b, c):
                pe.wait_ge(xhat_done, TB * (b.n + 1))
                for t in range(TB):
                    mm = nc.tensor.transpose(ps_y[c][:, t * P:(t + 1) * P], xhat[:, t, c * P:(c + 1) * P], ident[:])
                mm.then_inc(xhT_ps, 1)

            def project_q1(b, _):
                pe.wait_ge(xhT_done, EC * (b.n + 1))
                for c in range(EC):
                    mm = nc.tensor.matmul(ps_q1, a1_gamma[:, c, :], xhT[:, c, :], start=(c == 0), stop=(c == EC - 1))
                mm.then_inc(qw1_ps, 1)

            def scores1(b, i):
                t, k = i // len(chunks), i % len(chunks)
                if i == 0:
                    pe.wait_ge(qw1_lo_done, b.n + 1)
                elif k % 2 == 0 and t > 0:
                    pe.wait_ge(exp1_done, 2 * (TB * b.n + t) - 1 + k // 2)
                q = slice(t * P, (t + 1) * P)
                lo, hi = chunks[k]
                split3(ps_s1[:, lo:hi], qw1_hi[:, q], qw1_lo[:, q], ctxT_hi[b.par][:, lo:hi],
                       ctxT_lo[b.par][:, lo:hi]).then_inc(s1_ps, 1)

            def turn_p1(b, i):
                if i == 0:
                    pe.wait_ge(exp1_done, 2 * TB * (b.n + 1))
                elif i >= 3:
                    pe.wait_ge(p1T_lo_done, MT * b.n + i - 2)
                m = rows(i)
                for t in range(TB):
                    mm = nc.tensor.transpose(ps_turn[i % 3][0:m, t * P:(t + 1) * P], p1[:, t, i * P:i * P + m], ident[:])
                mm.then_inc(p1T_ps, 1)

            def weigh1(b, i):
                pe.wait_ge(p1T_lo_done, MT * b.n + i + 1)
                m = rows(i)
                split3(ps_acc1, ctx_hi[b.par][0:m, i, :], ctx_lo[b.par][0:m, i, :], p1T_hi[0:m, i % RING, :],
                       p1T_lo[0:m, i % RING, :], start=(i == 0), stop=(i == MT - 1)).then_inc(pv1_ps, 1)

            def project_out(b, h):
                if h == 0:
                    pe.wait_ge(at1_done, b.n + 1)
                for k in range(2):
                    t = slice((2 * h + k) * P, (2 * h + k + 1) * P)
                    mm = nc.tensor.matmul(ps_out[h][:, k * E:(k + 1) * E], at1[:, t], w2_sb[:], start=True, stop=True)
                mm.then_inc(out_ps, 1)

            def pre():
                pe.wait_ge(ident_done, 1)
                pe.wait_ge(cols_loaded, 16 * NV)
                for c in range(EC):
                    mm = nc.tensor.transpose(ps_misc[:, c * NV:(c + 1) * NV], vec_rows[:, c * P:(c + 1) * P],
                                             ident[0:NV, 0:NV])
                mm.then_inc(cols_turned, 1)
                pe.wait_ge(w_loaded, 16 * 4)
                for n in range(2):
                    for h in range(EC):
                        for c in range(EC):
                            mm = nc.tensor.transpose(ps_s0[:, n, h * E + c * P:h * E + (c + 1) * P],
                                                     wq_sb[n][:, c, h * P:(h + 1) * P], ident[:])
                    mm.then_inc(wT_turned, 1)
                for n in range(2):
                    for h in range(EC):
                        mm = nc.tensor.transpose(s1_bank(0)[:, (2 * n + h) * P:(2 * n + h + 1) * P],
                                                 wk_sb[n][:, h * P:(h + 1) * P], ident[:])
                mm.then_inc(wT_turned, 1)
                pe.wait_ge(wv_loaded, 16 * 3)
                for h in range(EC):
                    mm = nc.tensor.transpose(s1_bank(1)[:, h * P:(h + 1) * P], wv1_sb[:, h * P:(h + 1) * P], ident[:])
                mm.then_inc(wT_turned, 1)
                pe.wait_ge(wT_copied, 4)
                for n in range(2):
                    for c in range(EC):
                        for h in range(EC):
                            mm = nc.tensor.matmul(s1_bank(2)[:, (2 * n + c) * P:(2 * n + c + 1) * P],
                                                  wqT[n][:, h, c * P:(c + 1) * P], wkT[:, n, h, :],
                                                  start=(h == 0), stop=(h == EC - 1))
                mm.then_inc(made_ps, 1)
                pe.wait_ge(reps_done, 3 * EC)
                for c in range(EC):
                    for h in range(EC):
                        nc.tensor.matmul(s1_bank(3)[:, c * P:(c + 1) * P], wqT[0][:, h, c * P:(c + 1) * P],
                                         bk_rep[0][:, h, :], start=(h == 0), stop=(h == EC - 1))
                for h in range(EC):
                    mm = nc.tensor.matmul(s1_bank(3)[:, E:2 * E], bk_rep[1][:, h, :], wqT[1][:, h, :],
                                          start=(h == 0), stop=(h == EC - 1))
                mm.then_inc(made_ps, 1)
                for h in range(EC):
                    nc.tensor.matmul(ps_acc0[:, 0:E], wvT[:, h, :], wo_sb[:, h, :], start=(h == 0), stop=(h == EC - 1))
                for h in range(EC):
                    mm = nc.tensor.matmul(ps_acc0[:, E:2 * E], bv1_rep[:, h, :], wo_sb[:, h, :],
                                          start=(h == 0), stop=(h == EC - 1))
                mm.then_inc(made_ps, 1)
                for n in range(2):
                    for h in range(EC):
                        nc.tensor.matmul(ps_misc[:, 2 + n:3 + n], bk_rep[n][:, h, :], bq_col[n][:, h:h + 1],
                                         start=(h == 0), stop=(h == EC - 1))
                for h in range(EC):
                    nc.tensor.matmul(ps_misc[:, 0:1], wkT[:, 0, h, :], bq_col[0][:, h:h + 1],
                                     start=(h == 0), stop=(h == EC - 1))
                pe.wait_ge(a_copied, 1)
                for h in range(EC):
                    nc.tensor.matmul(ps_misc[:, 1:2], wkT[:, 1, h, :], bq_col[1][:, h:h + 1], start=(h == 0), stop=False)
                for c in range(EC):
                    mm = nc.tensor.matmul(ps_misc[:, 1:2], a_sb[:, 1, c, :], beta_col[:, c:c + 1], start=False,
                                          stop=(c == EC - 1))
                mm.then_inc(small_ps, 1)
                pe.wait_ge(small_sb, 1)
                pe.wait_ge(made_sb, 3)
                pe.wait_ge(pad_done, MADE)

            MISC = ("turn_x", "project_q0", "project_bias0", "turn_ctx", "predict")

            def misc_read(step, a, b, c):
                here = [(n, {"a": a, "b": b, "c": c}[who], i) for n, who, i in TENSOR_ORDER[:step] if n in MISC]
                before = [(n, {"a": b, "c": a}[who], i) for n, who, i in TENSOR_ORDER if n in MISC]
                for n, bt, i in reversed(before + here):
                    if bt:
                        break
                else:
                    return
                if n == "turn_x":
                    pe.wait_ge(xT_done, EC * bt.n + i + 1)
                elif n == "project_q0":
                    pe.wait_ge(qw0_lo_done, bt.n + 1)
                elif n == "project_bias0":
                    pe.wait_ge(cb_done, bt.n + 1)
                elif n == "turn_ctx":
                    pe.wait_ge(ctxT_lo_done, GROUPS * bt.n + i + 1)
                else:
                    pe.wait_ge(xr_done, 2 * bt.n + i + 1)

            steps = {f.__name__: f for f in (
                turn_x, project_q0, project_bias0, turn_ctx, scores0, weigh0, predict, turn_y, project_q1, scores1, turn_p1, weigh1, project_out)}

            def body(a, b, c):
                for step, (name, who, i) in enumerate(TENSOR_ORDER):
                    bt = {"a": a, "b": b, "c": c}[who]
                    if bt:
                        if name in MISC:
                            misc_read(step, a, b, c)
                        steps[name](bt, i)

            run(body, pre, pe)

        @blk.scalar
        def _(act):
            def ctx_high(a, g):
                act.wait_ge(ctxT_ps, GROUPS * a.n + g + 1)
                lo, hi = group_cols(g)
                nc.scalar.copy(ctxT_hi[a.par][:, lo:hi], ps_misc[:, 0:hi - lo]).then_inc(ctxT_hi_done, 1)

            def ctx_split(a, g):
                act.wait_ge(ctx_loaded[g], 16 * (a.n + 1))
                if g == 0 and not (isinstance(a.n, int) and a.n < 2):
                    act.wait_ge(pv1_ps, MT * (a.n - 2) + group(g)[-1] + 1)
                m = rows(group(g)[0])
                tiles = slice(group(g)[0], group(g)[-1] + 1)
                nc.scalar.copy(ctx_hi[a.par][0:m, tiles, :], ctx_sb[0:m, tiles, :]).then_inc(ctx_hi_done, 1)

            def x_turned(a, c):
                act.wait_ge(xT_ps, EC * a.n + c + 1)
                if c == 0 and not first(a):
                    act.wait_ge(cb_ps, a.n)
                nc.scalar.copy(xT[:, c, :], ps_misc[:]).then_inc(xT_done, 1)

            def q0_high(a, _):
                act.wait_ge(qw0_ps, a.n + 1)
                nc.scalar.activation(qw0_hi[a.par][:], ps_misc[:], ACT.Identity, bias=qb0, scale=1.0
                                     ).then_inc(qw0_hi_done, 1)

            def bias0(a, _):
                act.wait_ge(cb_ps, a.n + 1)
                nc.scalar.activation(cb[a.par][:], ps_misc[:], ACT.Identity, bias=bqbk0, scale=1.0
                                     ).then_inc(cb_done, 1)

            def exp0(a, i):
                act.wait_ge(s0_read, MT * a.n + i + 1)
                if (n := before0(a, i)) is not None:
                    act.wait_ge(p0_lo_done, n)
                m = rows(i)
                nc.scalar.activation(p0[0:m, ring0(i), :], s0_sb[0:m, (a.par + i) % 2, :], ACT.Exp, bias=min0[0:m, i:i + 1],
                                     scale=-1.0, accum_out=sum0[0:m, i:i + 1]).then_inc(exp0_done, 1)

            def p0_high(a, i):
                act.wait_ge(r0_done, MT * a.n + i + 1)
                if (n := before0(a, i)) is not None:
                    act.wait_ge(pv0_ps, n)
                    act.wait_ge(wsum_done, n)
                m = rows(i)
                nc.scalar.activation(p0_hi[0:m, ring0(i), :], p0[0:m, ring0(i), :], ACT.Copy, scale=r0[0:m, i:i + 1]
                                     ).then_inc(p0_hi_done, 1)

            def weighed0(a, _):
                act.wait_ge(pv0_ps, MT * (a.n + 1))
                if not first(a):
                    act.wait_ge(pred_ps, 2 * a.n)
                nc.scalar.copy(at0[:], ps_acc0[:]).then_inc(at0_done, 1)

            def y_turned(b, c):
                act.wait_ge(xhT_ps, EC * b.n + c + 1)
                nc.scalar.copy(xhT[:, c, :], ps_y[c]).then_inc(xhT_done, 1)

            def q1_high(b, _):
                act.wait_ge(qw1_ps, b.n + 1)
                nc.scalar.activation(qw1_hi[:], ps_q1, ACT.Identity, bias=scaled1[:, 0:1], scale=1.0
                                     ).then_inc(qw1_hi_done, 1)

            def exp1(b, i):
                t, h = i // 2, i % 2
                if h == 0:
                    act.wait_ge(bias1_done, TB * b.n + t + 1)
                part = halves[h]
                nc.scalar.activation(p1[:, t, part], ps_s1[:, part], ACT.Exp, bias=bias1[:, t:t + 1], scale=1.0,
                                     accum_out=sum1[:, h, t:t + 1]).then_inc(exp1_done, 1)

            def p1_turned(b, i):
                act.wait_ge(p1T_ps, MT * b.n + i + 1)
                if i >= RING:
                    act.wait_ge(pv1_ps, MT * b.n + i + 1 - RING)
                m = rows(i)
                nc.scalar.copy(p1T_hi[0:m, i % RING, :], ps_turn[i % 3][0:m, :]).then_inc(p1T_hi_done, 1)

            def weighed1(b, _):
                act.wait_ge(pv1_ps, MT * (b.n + 1))
                nc.scalar.copy(at1[:], ps_acc1).then_inc(at1_done, 1)

            def pre():
                for n, v in enumerate((bq0, bk0, bq1, bk1, bv1, gamma, beta)):
                    act.dma_start(vec_rows[n:n + 1, :], v.rearrange("(o e) -> o e", o=1)).then_inc(cols_loaded, 16)
                act.dma_start(wv0_sb[:], wv0).then_inc(wv_loaded, 16)
                act.dma_start(wv1_sb, wv1).then_inc(wv_loaded, 16)
                act.dma_start(wo_sb, wo.rearrange("(c p) d -> p c d", p=P)).then_inc(wv_loaded, 16)
                for row, v, landed in ((bv0_row, bv0, rows_loaded), (gamma_row, gamma, rows_loaded),
                                       (beta_row, beta, out_free[0]), (bo_row, bo, out_free[1])):
                    act.dma_start(row[:], v.rearrange("(o e) -> o e", o=1).broadcast_to([P, E])).then_inc(landed, 16)
                for n in range(2):
                    act.wait_ge(wT_turned, n + 1)
                    nc.scalar.copy(wqT[n].rearrange("p h e -> p (h e)"), ps_s0[:, n, :]).then_inc(wT_copied, 1)
                act.wait_ge(wT_turned, 3)
                nc.scalar.copy(wkT.rearrange("p n h l -> p (n h l)"), s1_bank(0)).then_inc(wT_copied, 1)
                act.wait_ge(wT_turned, 4)
                nc.scalar.copy(wvT.rearrange("p h l -> p (h l)"), s1_bank(1)[:, 0:E]).then_inc(wT_copied, 1)
                act.wait_ge(made_ps, 1)
                nc.scalar.copy(a_sb[:].rearrange("p n c l -> p (n c l)"), s1_bank(2)).then_inc(a_copied, 1)
                act.wait_ge(made_ps, 2)
                nc.scalar.copy(u0_rep[:].rearrange("p c l -> p (c l)"), s1_bank(3)[:, 0:E]).then_inc(made_sb, 1)
                nc.scalar.copy(u1_row[:], s1_bank(3)[:, E:2 * E]).then_inc(made_sb, 1)
                act.wait_ge(made_ps, 3)
                nc.scalar.copy(w2_sb[:], ps_acc0[:, 0:E]).then_inc(made_sb, 1)
                act.wait_ge(small_ps, 1)
                nc.scalar.copy(small[:], ps_misc[:, 0:4]).then_inc(small_sb, 1)
                act.wait_ge(small_sb, 1)
                act.wait_ge(pad_done, MADE)

            steps = {f.__name__: f for f in (
                x_turned, q0_high, bias0, ctx_high, ctx_split, exp0, p0_high, weighed0, y_turned, q1_high, exp1, p1_turned, weighed1)}

            def body(a, b, c):
                for name, who, i in SCALAR_ORDER:
                    bt = {"a": a, "b": b, "c": c}[who]
                    if bt:
                        steps[name](bt, i)

            run(body, pre, act)

        @blk.vector
        def _(dve):
            def ctx_low(a, g):
                dve.wait_ge(ctxT_hi_done, GROUPS * a.n + g + 1)
                lo, hi = group_cols(g)
                nc.vector.tensor_tensor(ctxT_lo[a.par][:, lo:hi], ps_misc[:, 0:hi - lo],
                                        ctxT_hi[a.par][:, lo:hi].bitcast(F32), ALU.subtract).then_inc(ctxT_lo_done, 1)

            def q0_low(a, _):
                dve.wait_ge(qw0_hi_done, a.n + 1)
                nc.vector.scalar_tensor_tensor(qw0_lo[a.par][:], ps_misc[:], qb0, qw0_hi[a.par][:].bitcast(F32),
                                               ALU.add, ALU.subtract).then_inc(qw0_lo_done, 1)

            def max0(a, i):
                if i == 0:
                    dve.wait_ge(cb_done, a.n + 1)
                if i >= 2 or not first(a):
                    dve.wait_ge(exp0_done, MT * a.n + i - 1)
                wait_apart(dve, s0_ps, MT * a.n + i + 1)
                m = rows(i)
                nc.vector.tensor_tensor_reduce(out=s0_sb[0:m, (a.par + i) % 2, :], in0=ps_s0[0:m, (a.par + i) % 2, :], in1=cb[a.par][0:m, :],
                                               scale=-SCALE, scalar=BIG, op0=ALU.add, op1=ALU.min,
                                               accum_out=min0[0:m, i:i + 1]).then_inc(s0_read, 1)

            def recip0(a, i):
                dve.wait_ge(exp0_done, MT * a.n + i + 1)
                m = rows(i)
                nc.vector.reciprocal(r0[0:m, i:i + 1], sum0[0:m, i:i + 1]).then_inc(r0_done, 1)

            def p0_low(a, i):
                dve.wait_ge(p0_hi_done, MT * a.n + i + 1)
                m = rows(i)
                nc.vector.scalar_tensor_tensor(p0_lo[0:m, ring0(i), :], p0[0:m, ring0(i), :], r0[0:m, i:i + 1],
                                               p0_hi[0:m, ring0(i), :].bitcast(F32), ALU.mult, ALU.subtract
                                               ).then_inc(p0_lo_done, 1)

            def p1_low(b, i):
                dve.wait_ge(p1T_hi_done, MT * b.n + i + 1)
                m = rows(i)
                nc.vector.tensor_tensor(p1T_lo[0:m, i % RING, :], ps_turn[i % 3][0:m, :],
                                        p1T_hi[0:m, i % RING, :].bitcast(F32), ALU.subtract).then_inc(p1T_lo_done, 1)

            def residual0(a, h):
                two = slice(2 * h, 2 * h + 2)
                dve.wait_ge(pred_ps, 2 * a.n + h + 1)
                nc.vector.tensor_tensor(xr[:, two, :], ps_misc[:].rearrange("p (t e) -> p t e", e=E),
                                        x_sb[a.par][:, two, :], ALU.add).then_inc(xr_done, 1)

            def moments0(a, h):
                two = slice(2 * h, 2 * h + 2)
                dve.wait_ge(xr_done, 2 * a.n + h + 1)
                for t in (2 * h, 2 * h + 1):
                    nc.vector.bn_stats(stats[:, t, :], xr[:, t, :]).then_inc(stats_done, 1)
                for t in (2 * h, 2 * h + 1):
                    wait_apart(dve, stats_done, TB * a.n + t + 1)
                    nc.vector.bn_aggr(mv[:, t, :], stats[:, t, :]).then_inc(mv_done, 1)
                dve.wait_ge(mv_done, TB * a.n + 2 * h + 2)
                nc.vector.tensor_scalar(var_eps[:, two, :], mv[:, two, 1:2], LN_EPS, None, ALU.add).then_inc(var_done, 1)

            def normalised(a, h):
                dve.wait_ge(rstd_done, 2 * a.n + h + 1)
                if h == 0 and not first(a):
                    dve.wait_ge(xhT_ps, EC * a.n)
                    dve.wait_ge(y_part_done, a.n)
                for t in (2 * h, 2 * h + 1):
                    nc.vector.tensor_scalar(xhat[:, t, :], xr[:, t, :], mv[:, t, 0:1], rstd[:, t, :], ALU.subtract,
                                            ALU.mult).then_inc(xhat_done, 1)

            def bias_row1(b, _):
                dve.wait_ge(xhat_done, TB * (b.n + 1))
                for t in range(TB):
                    nc.vector.tensor_tensor_reduce(out=junk[:, t, :], in0=xhat[:, t, :], in1=u1_gamma[:], scale=1.0,
                                                   scalar=c1_const[:, 0:1], op0=ALU.mult, op1=ALU.add,
                                                   accum_out=c1[:, t:t + 1]).then_inc(c1_done, 1)

            def q1_low(b, _):
                dve.wait_ge(qw1_hi_done, b.n + 1)
                nc.vector.scalar_tensor_tensor(qw1_lo[:], ps_q1, scaled1[:, 0:1], qw1_hi[:].bitcast(F32), ALU.add,
                                               ALU.subtract).then_inc(qw1_lo_done, 1)

            def rowmax1(b, i):
                t, k = i // len(chunks), i % len(chunks)
                lo, hi = chunks[k]
                dve.wait_ge(s1_ps, len(chunks) * TB * b.n + i + 1)
                nc.vector.tensor_reduce(max1[:, t, k:k + 1], ps_s1[:, lo:min(hi, M)], AX_X, ALU.max
                                        ).then_inc(max1_done, 1)

            def bias1_of(b, t):
                if t == 0:
                    dve.wait_ge(c1_done, TB * (b.n + 1))
                dve.wait_ge(max1_done, len(chunks) * (TB * b.n + t + 1))
                nc.vector.tensor_reduce(neg_max1[:, t:t + 1], max1[:, t, :], AX_X, ALU.max, negate=True
                                        ).then_inc(neg_max1_done, 1)
                dve.wait_ge(neg_max1_done, TB * b.n + t + 1)
                nc.vector.scalar_tensor_tensor(bias1[:, t:t + 1], neg_max1[:, t:t + 1], c1[:, t:t + 1], c1[:, t:t + 1],
                                               ALU.subtract, ALU.add).then_inc(bias1_done, 1)

            def recip1(b, _):
                dve.wait_ge(exp1_done, 2 * TB * (b.n + 1))
                nc.vector.tensor_tensor(sum1_all[:], sum1[:, 0, :], sum1[:, 1, :], ALU.add).then_inc(sum1_done, 1)
                dve.wait_ge(sum1_done, b.n + 1)
                nc.vector.reciprocal(r1[:], sum1_all[:]).then_inc(r1_done, 1)

            def finish(b, h):
                if h == 0:
                    dve.wait_ge(r1_done, b.n + 1)
                    dve.wait_ge(y_res_done, b.n + 1)
                dve.wait_ge(out_free[h], 16 * (b.n + 1))
                dve.wait_ge(out_ps, 2 * b.n + h + 1)
                for k in range(2):
                    t = 2 * h + k
                    ins = nc.vector.scalar_tensor_tensor(o_sb[:, t, :], ps_out[h][:, k * E:(k + 1) * E], r1[:, t:t + 1],
                                                         y_res[:, t, :], ALU.mult, ALU.add)
                ins.then_inc(o_done, 1)

            def pre():
                for p in range(2):
                    nc.vector.memset(ctxT_hi[p][:, M:MPAD].bitcast(F32), 0.0)
                    nc.vector.memset(ctxT_lo[p][:, M:MPAD].bitcast(F32), 0.0)
                nc.vector.memset(ones[:], 1.0).then_inc(ones_done, 1)
                dve.wait_ge(ones_done, 1)
                dve.wait_ge(cols_turned, 1)
                nc.vector.tensor_copy(cols[:].rearrange("p c n -> p (c n)"), ps_misc[:, 0:EC * NV]).then_inc(cols_done, 1)
                dve.wait_ge(cols_done, 1)
                for rep, col in ((bk_rep[0], bk_col[0]), (bk_rep[1], bk_col[1]), (bv1_rep, bv1_col)):
                    for h in range(EC):
                        nc.vector.tensor_scalar(rep[:, h, :], ones[:], col[:, h:h + 1], None, ALU.mult
                                                ).then_inc(reps_done, 1)
                dve.wait_ge(rows_loaded, 16 * 2)
                for h in range(2):
                    dve.wait_ge(out_free[h], 16)
                dve.wait_ge(a_copied, 1)
                for c in range(EC):
                    nc.vector.tensor_scalar(a1_gamma[:, c, :], a_sb[:, 1, c, :], gamma_col[:, c:c + 1], SCALE, ALU.mult, ALU.mult
                                            ).then_inc(pad_done, 1)
                nc.vector.tensor_tensor(betaob_part[:], beta_row[:], bo_row[:], ALU.add).then_inc(pad_done, 1)
                dve.wait_ge(made_sb, 3)
                dve.wait_ge(pad_done, 3)
                nc.vector.tensor_tensor(betaob_row[:], ps_acc0[:, E:2 * E], betaob_part[:], ALU.add).then_inc(pad_done, 1)
                dve.wait_ge(small_sb, 1)
                nc.vector.scalar_tensor_tensor(u1_gamma[:], u1_row[:], SCALE, gamma_row[:], ALU.mult, ALU.mult
                                               ).then_inc(pad_done, 1)
                nc.vector.tensor_scalar(scaled1[:], small[:, 1:4:2], SCALE, None, ALU.mult).then_inc(pad_done, 1)
                dve.wait_ge(pad_done, 6)
                nc.vector.tensor_tensor_reduce(out=junk[:, 0, :], in0=u1_row[:], in1=beta_row[:], scale=SCALE,
                                               scalar=scaled1[:, 1:2], op0=ALU.mult, op1=ALU.add,
                                               accum_out=c1_const[:, 0:1]).then_inc(pad_done, 1)
                dve.wait_ge(pad_done, MADE)

            steps = {f.__name__: f for f in (
                ctx_low, q0_low, max0, recip0, p0_low, residual0, moments0, normalised, bias_row1, q1_low, rowmax1, bias1_of, recip1, p1_low, finish)}

            def body(a, b, c):
                for name, who, i in VECTOR_ORDER:
                    bt = {"a": a, "b": b, "c": c}[who]
                    if bt:
                        steps[name](bt, i)

            run(body, pre, dve)

        @blk.gpsimd
        def _(pool):
            def ctx_low(a, g):
                pool.wait_ge(ctx_hi_done, GROUPS * a.n + g + 1)
                m = rows(group(g)[0])
                tiles = slice(group(g)[0], group(g)[-1] + 1)
                nc.gpsimd.tensor_tensor(ctx_lo[a.par][0:m, tiles, :], ctx_sb[0:m, tiles, :],
                                        ctx_hi[a.par][0:m, tiles, :].bitcast(F32), ALU.subtract).then_inc(ctx_lo_done, 1)

            def sum_weights(a, i):
                pool.wait_ge(p0_lo_done, MT * a.n + i + 1)
                m = rows(i)
                total = wsum[a.par][0:m, :]
                hi, lo = (part[0:m, ring0(i), :].bitcast(F32) for part in (p0_hi, p0_lo))
                if i == 0:
                    nc.gpsimd.tensor_tensor(total, hi, lo, ALU.add).then_inc(wsum_done, 1)
                else:
                    pool.wait_ge(wsum_done, MT * a.n + i)
                    nc.gpsimd.tensor_tensor(total, total, lo, ALU.add).then_inc(wsum_part, 1)
                    pool.wait_ge(wsum_part, (MT - 1) * a.n + i)
                    nc.gpsimd.tensor_tensor(total, total, hi, ALU.add).then_inc(wsum_done, 1)

            def residual1(b, _):
                pool.wait_ge(xhat_done, TB * (b.n + 1))
                pool.wait_ge(c1_done, TB * (b.n + 1))
                for t in range(TB):
                    ins = nc.gpsimd.tensor_tensor(y_res[:, t, :], xhat[:, t, :], gamma_row[:], ALU.mult)
                ins.then_inc(y_part_done, 1)
                pool.wait_ge(y_part_done, b.n + 1)
                for t in range(TB):
                    ins = nc.gpsimd.tensor_tensor(y_res[:, t, :], y_res[:, t, :], betaob_row[:], ALU.add)
                ins.then_inc(y_res_done, 1)

            def rsqrt_var(a, h):
                pool.wait_ge(var_done, 2 * a.n + h + 1)
                two = slice(2 * h, 2 * h + 2)
                nc.gpsimd.tensor_tensor(rstd[:, two, :], var_eps[:, two, :], neg_half[:], ALU.pow).then_inc(rstd_done, 1)

            def pre():
                nc.gpsimd.memset(neg_half[:], -0.5)
                nc.gpsimd.memset(ident[:], 0.0).then_inc(ident_zero, 1)
                pool.wait_ge(ident_zero, 1)
                nc.gpsimd.affine_select(out=ident[:], in_=ident[:], compare_op=ALU.not_equal, fill=1.0, base=0,
                                        pattern=[[-1, P]], channel_multiplier=1).then_inc(ident_done, 1)
                pool.wait_ge(rows_loaded, 16 * 2)
                pool.wait_ge(pad_done, MADE)

            steps = {f.__name__: f for f in (
                ctx_low, sum_weights, rsqrt_var, residual1)}

            def body(a, b, c):
                for name, who, i in GPSIMD_ORDER:
                    bt = {"a": a, "b": b, "c": c}[who]
                    if bt:
                        steps[name](bt, i)

            run(body, pre, pool)


_INS = ["x", "ctx_512"] + [f"L0_xattn_{n}" for n in ("Wq", "bq", "Wk", "bk", "Wv", "bv", "gamma", "beta")] + [
    f"L1_xattn_{n}" for n in ("Wq", "bq", "Wk", "bk", "Wv", "bv", "Wo", "bo")]


def kernel(**inputs):
    import numpy as np
    import concourse.bacc as bacc
    from concourse.bass_utils import run_bass_kernel_spmd

    nc = bacc.Bacc("TRN2", target_bir_lowering=False, num_devices=1)
    arrays, args = {}, []
    for name in _INS:
        a = np.ascontiguousarray(inputs[name])
        arrays[f"in_{name}_dram"] = a
        args.append(nc.dram_tensor(f"in_{name}_dram", a.shape, mybir.dt.from_np(a.dtype), kind="ExternalInput").ap())
    shape = inputs["x"].shape
    args.append(nc.dram_tensor("out_dram", shape, F32, kind="ExternalOutput").ap())
    xattn_kernel(nc, *args)
    r = run_bass_kernel_spmd(nc, [arrays], core_ids=[0])
    return r.results[0]["out_dram"]
```

```python
from collections import namedtuple
from contextlib import ExitStack

import concourse.bass as bass
from concourse import mybir

ALU = mybir.AluOpType
ACT = mybir.ActivationFunctionType
F32 = mybir.dt.float32
F32R = mybir.dt.float32r
AX_X = mybir.AxisListType.X

P = 128
BANK = 512
LN_EPS = 1e-6
BIG = 3.0e38

TENSOR_ORDER = (
    ("weigh0", "a", 3), ("turn_x", "c", 0), ("scores1", "b", 0), ("scores1", "b", 1), ("scores1", "b", 2),
    ("scores1", "b", 3), ("scores0", "a", 7), ("scores0", "a", 8), ("turn_x", "c", 1), ("weigh0", "a", 4),
    ("scores1", "b", 4), ("scores1", "b", 5), ("scores1", "b", 6), ("scores1", "b", 7), ("scores0", "a", 9),
    ("project_q0", "c", 0), ("scores1", "b", 8), ("scores1", "b", 9), ("scores1", "b", 10), ("scores1", "b", 11),
    ("weigh0", "a", 5), ("scores0", "a", 10), ("turn_ctx", "a", 3), ("weigh0", "a", 6), ("scores1", "b", 12),
    ("scores1", "b", 13), ("scores1", "b", 14), ("scores1", "b", 15), ("weigh0", "a", 7), ("project_bias0", "c", 0),
    ("scores0", "a", 11), ("turn_p1", "b", 0), ("turn_p1", "b", 1), ("turn_ctx", "c", 0), ("turn_p1", "b", 2),
    ("weigh0", "a", 8), ("scores0", "a", 12), ("weigh0", "a", 9), ("weigh1", "b", 0), ("turn_p1", "b", 3),
    ("turn_p1", "b", 4), ("weigh1", "b", 1), ("scores0", "c", 0), ("turn_ctx", "c", 1), ("turn_p1", "b", 5),
    ("scores0", "c", 1), ("weigh1", "b", 2), ("turn_p1", "b", 6), ("weigh0", "a", 10), ("turn_p1", "b", 7),
    ("turn_p1", "b", 8), ("weigh1", "b", 3), ("turn_p1", "b", 9), ("scores0", "c", 2), ("weigh0", "a", 11),
    ("weigh1", "b", 4), ("weigh1", "b", 5), ("weigh1", "b", 6), ("sum_rows0", "a", 0), ("weigh1", "b", 7),
    ("weigh0", "a", 12), ("scores0", "c", 3), ("turn_p1", "b", 10), ("turn_p1", "b", 11), ("predict", "a", 0),
    ("weigh1", "b", 8), ("weigh0", "c", 0), ("predict", "a", 1), ("scores0", "c", 4), ("turn_p1", "b", 12),
    ("weigh1", "b", 9), ("weigh1", "b", 10), ("scores0", "c", 5), ("weigh1", "b", 11), ("weigh1", "b", 12),
    ("turn_ctx", "c", 2), ("weigh0", "c", 1), ("project_out", "b", 0), ("project_out", "b", 1), ("turn_y", "a", 0),
    ("turn_y", "a", 1), ("scores0", "c", 6), ("project_q1", "a", 0), ("weigh0", "c", 2),
)
SCALAR_ORDER = (
    ("p0_high", "a", 5), ("ctx_split", "a", 2), ("exp0", "a", 6), ("p0_high", "a", 6), ("x_turned", "c", 0),
    ("exp1", "b", 0), ("exp0", "a", 7), ("exp1", "b", 1), ("x_turned", "c", 1), ("p0_high", "a", 7), ("exp0", "a", 8),
    ("exp1", "b", 2), ("exp1", "b", 3), ("p0_high", "a", 8), ("q0_high", "c", 0), ("exp0", "a", 9), ("exp1", "b", 4),
    ("p0_high", "a", 9), ("exp1", "b", 5), ("ctx_high", "a", 3), ("exp1", "b", 6), ("exp1", "b", 7),
    ("bias0", "c", 0), ("exp0", "a", 10), ("ctx_high", "c", 0), ("p1_turned", "b", 0), ("p1_turned", "b", 1),
    ("p0_high", "a", 10), ("exp0", "a", 11), ("p1_turned", "b", 2), ("ctx_split", "a", 3), ("p0_high", "a", 11),
    ("p1_turned", "b", 3), ("exp0", "a", 12), ("p1_turned", "b", 4), ("p1_turned", "b", 5), ("exp0", "c", 0),
    ("p1_turned", "b", 6), ("p0_high", "a", 12), ("p0_high", "c", 0), ("ctx_high", "c", 1), ("p1_turned", "b", 7),
    ("exp0", "c", 1), ("ctx_split", "c", 0), ("p0_high", "c", 1), ("exp0", "c", 2), ("p1_turned", "b", 8),
    ("p1_turned", "b", 9), ("weighed0", "a", 0), ("p1_turned", "b", 10), ("p0_high", "c", 2), ("exp0", "c", 3),
    ("p1_turned", "b", 11), ("p1_turned", "b", 12), ("p0_high", "c", 3), ("exp0", "c", 4), ("weighed1", "b", 0),
    ("p0_high", "c", 4), ("exp0", "c", 5), ("ctx_high", "c", 2), ("ctx_split", "c", 1), ("y_turned", "a", 0),
    ("y_turned", "a", 1), ("q1_high", "a", 0),
)
VECTOR_ORDER = (
    ("max0", "a", 6), ("p0_low", "a", 5), ("rowmax1", "b", 0), ("recip0", "a", 6), ("rowmax1", "b", 1),
    ("rowmax1", "b", 2), ("rowmax1", "b", 3), ("bias1_of", "b", 0), ("max0", "a", 7), ("max0", "a", 8),
    ("p0_low", "a", 6), ("rowmax1", "b", 4), ("rowmax1", "b", 5), ("recip0", "a", 7), ("rowmax1", "b", 6),
    ("rowmax1", "b", 7), ("bias1_of", "b", 1), ("recip0", "a", 8), ("p0_low", "a", 7), ("max0", "a", 9),
    ("rowmax1", "b", 8), ("rowmax1", "b", 9), ("rowmax1", "b", 10), ("rowmax1", "b", 11), ("recip0", "a", 9),
    ("bias1_of", "b", 2), ("q0_low", "c", 0), ("p0_low", "a", 8), ("rowmax1", "b", 12), ("rowmax1", "b", 13),
    ("rowmax1", "b", 14), ("rowmax1", "b", 15), ("ctxT_low", "a", 3), ("bias1_of", "b", 3), ("max0", "a", 10),
    ("p0_low", "a", 9), ("recip1", "b", 0), ("recip0", "a", 10), ("max0", "a", 11), ("ctxT_low", "c", 0),
    ("p1_low", "b", 0), ("p1_low", "b", 1), ("p0_low", "a", 10), ("max0", "a", 12), ("recip0", "a", 11),
    ("p1_low", "b", 2), ("p0_low", "a", 11), ("max0", "c", 0), ("p1_low", "b", 3), ("recip0", "a", 12),
    ("p1_low", "b", 4), ("recip0", "c", 0), ("p1_low", "b", 5), ("max0", "c", 1), ("p1_low", "b", 6),
    ("p0_low", "a", 12), ("p0_low", "c", 0), ("p1_low", "b", 7), ("ctxT_low", "c", 1), ("recip0", "c", 1),
    ("max0", "c", 2), ("p0_low", "c", 1), ("recip0", "c", 2), ("p1_low", "b", 8), ("p1_low", "b", 9),
    ("bias_x0", "a", 0), ("max0", "c", 3), ("p1_low", "b", 10), ("residual0", "a", 0), ("recip0", "c", 3),
    ("moments0", "a", 0), ("p0_low", "c", 2), ("residual0", "a", 1), ("p1_low", "b", 11), ("max0", "c", 4),
    ("p1_low", "b", 12), ("moments0", "a", 1), ("normalised", "a", 0), ("recip0", "c", 4), ("max0", "c", 5),
    ("normalised", "a", 1), ("p0_low", "c", 3), ("finish", "b", 0), ("finish", "b", 1), ("p0_low", "c", 4),
    ("recip0", "c", 5), ("ctxT_low", "c", 2), ("bias_row1", "a", 0), ("q1_low", "a", 0),
)
GPSIMD_ORDER = (
    ("sum_weights", "a", 2), ("sum_weights", "a", 3), ("ctx_low", "a", 1), ("residual1", "b", 0),
    ("sum_weights", "a", 4), ("sum_weights", "a", 5), ("ctx_low", "a", 2), ("sum_weights", "a", 6),
    ("sum_weights", "a", 7), ("sum_weights", "a", 8), ("sum_weights", "a", 9), ("sum_weights", "a", 10),
    ("sum_weights", "a", 11), ("sum_weights", "a", 12), ("ctx_low", "a", 3), ("sum_weights", "c", 0),
    ("ctx_low", "c", 0), ("rsqrt_var", "a", 0), ("sum_weights", "c", 1), ("rsqrt_var", "a", 1),
)
WARM = (10, 2, 4)

Batch = namedtuple("Batch", "n use par")


def batch(pair, k):
    return Batch(2 * pair + k, pair + k // 2, k % 2)


def first(bt):
    return isinstance(bt.n, int) and bt.n == 0


def xattn_kernel(nc, x, ctx, wq0, bq0, wk0, bk0, wv0, bv0, gamma, beta,
                 wq1, bq1, wk1, bk1, wv1, bv1, wo, bo, out):
    B, T, E = x.shape
    _, M, L = ctx.shape
    TB = T // P
    EC = E // P
    MT = -(-M // P)
    MPAD = M + M % 2
    GROUPS = -(-MT // TB)
    SCALE = float(E) ** -0.5
    RING = 4

    def ring0(i):
        return 4 if i == MT - 1 else i % 4

    def before0(a, i):
        last = i - 4 if 4 <= i < MT - 1 else (i + 8 - MT if i < 4 else -1)
        if last < 0 and isinstance(a.n, int) and a.n == 0:
            return None
        return MT * a.n + last + 1

    PAIRS = (B - 2) // 2
    assert L == P and T == BANK and EC == 2 and TB == 4 and B % 2 == 0

    def rows(i):
        return min(P, M - i * P)

    def group(g):
        return range(TB * g, min(TB * g + TB, MT))

    def group_cols(g):
        return TB * g * P, min(M, TB * (g + 1) * P)

    CHUNK = -(-MPAD // 8) * 2
    chunks = [(c, min(MPAD, c + CHUNK)) for c in range(0, MPAD, CHUNK)]
    last_lo = chunks[-1][0]
    assert CHUNK <= BANK and len(chunks) == 4

    def last(bt):
        return isinstance(bt.n, int) and bt.n == B - 1

    with ExitStack() as stack:
        def sb(name, shape, dt=F32):
            return stack.enter_context(nc.sbuf_tensor(name, shape, dt))

        def sem(name):
            return stack.enter_context(nc.semaphore(name))

        p1 = sb("p1", [P, TB, M])
        p1_flat = p1[:].rearrange("p t m -> p (t m)")
        room = [0]

        def early(n):
            room[0] += n
            return p1_flat[:, room[0] - n:room[0]]

        ident = sb("ident", [P, P])
        ones = sb("ones", [P, P])
        wq_sb = [early(EC * E).rearrange("p (c h) -> p c h", c=EC) for _ in range(2)]
        wk_sb = [early(E) for _ in range(2)]
        wv0_sb = sb("wv0_sb", [P, E])
        wv1_sb = early(E)
        wo_sb = early(EC * E).rearrange("p (c d) -> p c d", c=EC)
        NV = [2, 5]
        vec_rows = [sb(f"vec_rows{n}", [NV[n], E]) for n in range(2)]
        cols = [sb(f"cols{n}", [P, EC, NV[n]]) for n in range(2)]
        bq_col = [cols[n][:, :, 0] for n in range(2)]
        bk_col = [cols[n][:, :, 1] for n in range(2)]
        bv1_col, gamma_col, beta_col = cols[1][:, :, 2], cols[1][:, :, 3], cols[1][:, :, 4]
        bv0_row = sb("bv0_row", [P, E])
        gamma_row = sb("gamma_row", [P, E])
        beta_row = sb("beta_row", [P, E])
        bo_row = sb("bo_row", [P, E])
        wqT = [early(EC * E).rearrange("p (h e) -> p h e", h=EC) for _ in range(2)]
        wkT = early(2 * EC * P).rearrange("p (n h l) -> p n h l", n=2, h=EC)
        wvT = early(EC * P).rearrange("p (h l) -> p h l", h=EC)
        bk_rep = [early(EC * P).rearrange("p (h l) -> p h l", h=EC) for _ in range(2)]
        bv1_rep = early(EC * P).rearrange("p (h l) -> p h l", h=EC)
        a_sb = sb("a_sb", [P, 2, EC, P])
        a1_gamma = sb("a1_gamma", [P, EC, P])
        u0_rep = sb("u0_rep", [P, EC, P])
        u1_row = sb("u1_row", [P, E])
        u1_gamma = sb("u1_gamma", [P, E])
        w2_sb = sb("w2_sb", [P, E])
        betaob_row = sb("betaob_row", [P, E])
        betaob_part = sb("betaob_part", [P, E])
        small = [sb(f"small{n}", [P, 2]) for n in range(2)]
        qb0 = small[0][:, 0:1]
        bqbk0 = small[0][:, 1:2]
        MADE = 7
        scaled1 = sb("scaled1", [P, 2])
        c1_const = sb("c1_const", [P, 1])
        junk = sb("junk", [P, TB, E])

        x_sb = [sb(f"x_sb{p}", [P, TB, E]) for p in range(2)]
        ctx_sb = sb("ctx_sb", [P, MT, L])
        ctx_hi = [sb(f"ctx_hi{p}", [P, MT, L], F32R) for p in range(2)]
        ctx_lo = [sb(f"ctx_lo{p}", [P, MT, L], F32R) for p in range(2)]
        ctxT_hi = [sb(f"ctxT_hi{p}", [P, MPAD], F32R) for p in range(2)]
        ctxT_lo = [sb(f"ctxT_lo{p}", [P, MPAD], F32R) for p in range(2)]
        xT = sb("xT", [P, EC, T])
        qw0_hi = [sb(f"qw0_hi{p}", [P, T], F32R) for p in range(2)]
        qw0_lo = [sb(f"qw0_lo{p}", [P, T], F32R) for p in range(2)]
        cb = [sb(f"cb{p}", [P, T]) for p in range(2)]
        s0_sb = sb("s0_sb", [P, 2, T])
        min0 = sb("min0", [P, MT])
        sum0 = sb("sum0", [P, MT])
        r0 = sb("r0", [P, MT])
        p0 = sb("p0", [P, 5, T])
        p0_hi = sb("p0_hi", [P, 5, T], F32R)
        p0_lo = sb("p0_lo", [P, 5, T], F32R)
        wsum = [sb(f"wsum{p}", [P, T]) for p in range(2)]
        rowsum0 = sb("rowsum0", [P, TB])
        at0 = sb("at0", [P, T])
        xr = sb("xr", [P, TB, E])
        stats = sb("stats", [P, TB, 6])
        mv = sb("mv", [P, TB, 2])
        var_eps = sb("var_eps", [P, TB, 1])
        rstd = sb("rstd", [P, TB, 1])
        neg_half = sb("neg_half", [P, 2, 1])
        xhat = sb("xhat", [P, TB, E])
        y_res = sb("y_res", [P, TB, E])
        xhT = xT
        qw1_hi = sb("qw1_hi", [P, T], F32R)
        qw1_lo = sb("qw1_lo", [P, T], F32R)
        c1 = sb("c1", [P, TB])
        max1 = sb("max1", [P, TB, len(chunks)])
        neg_max1 = sb("neg_max1", [P, TB])
        bias1 = sb("bias1", [P, TB])
        sum1 = sb("sum1", [P, 2, TB])
        sum1_all = sb("sum1_all", [P, TB])
        r1 = sb("r1", [P, TB])
        p1T_hi = sb("p1T_hi", [P, RING, T], F32R)
        p1T_lo = sb("p1T_lo", [P, RING, T], F32R)
        at1 = sb("at1", [P, T])
        o_sb = sb("o_sb", [P, TB, E])

        ps_l0 = stack.enter_context(nc.psum_tensor("ps_l0", [P, 4 * BANK], F32))
        ps_s1 = stack.enter_context(nc.psum_tensor("ps_s1", [P, 4 * BANK], F32))
        ps_s0 = ps_l0[:, 0:2 * BANK].rearrange("p (k t) -> p k t", t=BANK)
        ps_acc0 = ps_l0[:, 2 * BANK:3 * BANK]
        ps_misc = ps_l0[:, 3 * BANK:4 * BANK]

        def s1_bank(k):
            return ps_s1[:, k * BANK:(k + 1) * BANK]

        def s1_banks(b, t):
            return (ps_l0 if last(b) and t % 2 else ps_s1)[:].rearrange("p (k m) -> p k m", m=BANK)

        ps_turn = [s1_bank(k) for k in range(3)]
        ps_y = [s1_bank(0), s1_bank(3)]
        ps_q1 = s1_bank(0)
        ps_out = [s1_bank(1), s1_bank(2)]
        ps_acc1 = s1_bank(3)

        ident_zero, ident_done, ones_done = sem("ident_zero"), sem("ident_done"), sem("ones_done")
        row1_made = sem("row1_made")
        w_loaded = [sem(f"w_loaded{n}") for n in range(2)]
        cols_loaded = [sem(f"cols_loaded{n}") for n in range(2)]
        wv_loaded = sem("wv_loaded")
        rows_loaded = sem("rows_loaded")
        cols_turned, cols_done = sem("cols_turned"), sem("cols_done")
        wT_turned, wT_copied, reps_done = sem("wT_turned"), sem("wT_copied"), sem("reps_done")
        made_ps, a_copied, made_sb = sem("made_ps"), sem("a_copied"), sem("made_sb")
        small_ps, small_sb, beta_dot = sem("small_ps"), sem("small_sb"), sem("beta_dot")
        x_loaded = [sem(f"x_loaded{p}") for p in range(2)]
        ctx_loaded = [sem(f"ctx_loaded{g}") for g in range(GROUPS)]
        out_free = [sem(f"out_free{h}") for h in range(2)]
        ctxT_ps, xT_ps, qw0_ps, cb_ps = sem("ctxT_ps"), sem("xT_ps"), sem("qw0_ps"), sem("cb_ps")
        s0_ps, pv0_ps, pred_ps = sem("s0_ps"), sem("pv0_ps"), sem("pred_ps")
        rowsum_ps = sem("rowsum_ps")
        xhT_ps, qw1_ps, s1_ps, p1T_ps, pv1_ps, out_ps = (
            sem("xhT_ps"), sem("qw1_ps"), sem("s1_ps"), sem("p1T_ps"), sem("pv1_ps"), sem("out_ps"))
        ctxT_hi_done, xT_done, qw0_hi_done, cb_done = (
            sem("ctxT_hi_done"), sem("xT_done"), sem("qw0_hi_done"), sem("cb_done"))
        exp0_done, at0_done = sem("exp0_done"), sem("at0_done")
        xhT_done, qw1_hi_done, exp1_done, at1_done = (
            sem("xhT_done"), sem("qw1_hi_done"), sem("exp1_done"), sem("at1_done"))
        ctx_hi_done, p0_hi_done, p1T_hi_done = sem("ctx_hi_done"), sem("p0_hi_done"), sem("p1T_hi_done")
        ctxT_lo_done, qw0_lo_done, s0_read, r0_done = (
            sem("ctxT_lo_done"), sem("qw0_lo_done"), sem("s0_read"), sem("r0_done"))
        sum1_done = sem("sum1_done")
        rowsum_done, xbias_done = sem("rowsum_done"), sem("xbias_done")
        p0_lo_done, p1T_lo_done = sem("p0_lo_done"), sem("p1T_lo_done")
        xr_done, stats_done, mv_done, rstd_done, xhat_done = (
            sem("xr_done"), sem("stats_done"), sem("mv_done"), sem("rstd_done"), sem("xhat_done"))
        c1_done, qw1_lo_done, max1_done, neg_max1_done, bias1_done, r1_done, o_done = (
            sem("c1_done"), sem("qw1_lo_done"), sem("max1_done"), sem("neg_max1_done"), sem("bias1_done"),
            sem("r1_done"), sem("o_done"))
        var_done, wsum_part = sem("var_done"), sem("wsum_part")
        ctx_lo_done, wsum_done, y_part_done, y_res_done = (
            sem("ctx_lo_done"), sem("wsum_done"), sem("y_part_done"), sem("y_res_done"))

        apart_regs = {eng: eng.alloc_register("apart") for eng in (nc.vector, nc.gpsimd)}

        def wait_apart(eng, semaphore, value):
            if not isinstance(value, int):
                apart_reg = apart_regs[eng]
                eng.reg_mov(apart_reg, value)
                value = eng.snap(apart_reg, min_val=1)
            eng.wait_ge(ident_done, 1)
            eng.wait_ge(semaphore, value)

        blk = stack.enter_context(nc.Block())

        AHEAD = {("turn_x", 0), ("x_turned", 0), ("turn_x", 1), ("x_turned", 1),
                 ("turn_ctx", 0), ("ctx_high", 0), ("ctxT_low", 0)}

        def run(body, pre, eng):
            pre[0]()
            body(None, None, batch(0, 0), AHEAD)
            pre[1]()
            body(batch(0, 0), None, batch(0, 1))
            with eng.Fori(0, PAIRS) as pair:
                body(batch(pair, 1), batch(pair, 0), batch(pair, 2))
                body(batch(pair, 2), batch(pair, 1), batch(pair, 3))
            body(batch(PAIRS, 1), batch(PAIRS, 0), None)
            body(None, batch(PAIRS, 1), None)

        @blk.sync
        def _(sp):
            def load_x(c, after=None):
                if after is not None:
                    sp.wait_ge(xbias_done, c.n - 1)
                sp.dma_start(x_sb[c.par][:], x[bass.ds(c.n, 1)].rearrange("o (t p) e -> p (o t) e", p=P)
                             ).then_inc(x_loaded[c.par], 16)

            def load_ctx(c, g, after=None):
                if after is not None:
                    sp.wait_ge(ctxT_ps, GROUPS * (c.n - 1) + g + 1)
                    sp.wait_ge(ctx_lo_done, GROUPS * (c.n - 1) + g + 1)
                full = [i for i in group(g) if rows(i) == P]
                dst = ctx_sb
                if full:
                    src = ctx[bass.ds(c.n, 1), full[0] * P:(full[-1] + 1) * P, :]
                    sp.dma_start(dst[:, full[0]:full[-1] + 1, :], src.rearrange("o (i p) l -> p (o i) l", p=P)
                                 ).then_inc(ctx_loaded[g], 16)
                else:
                    i = group(g)[0]
                    src = ctx[bass.ds(c.n, 1), i * P:M, :]
                    sp.dma_start(dst[0:rows(i), i, :], src.rearrange("o p l -> (o p) l")
                                 ).then_inc(ctx_loaded[g], 16)

            def pre0():
                sp.dma_start(wq_sb[0], wq0.rearrange("(c p) h -> p c h", p=P)).then_inc(w_loaded[0], 16)
                sp.dma_start(wk_sb[0], wk0).then_inc(w_loaded[0], 16)
                load_x(batch(0, 0))
                for g in range(GROUPS):
                    load_ctx(batch(0, 0), g)
                sp.dma_start(wq_sb[1], wq1.rearrange("(c p) h -> p c h", p=P)).then_inc(w_loaded[1], 16)
                sp.dma_start(wk_sb[1], wk1).then_inc(w_loaded[1], 16)
                for k, v in enumerate((bq1, bk1, bv1, gamma, beta)):
                    sp.dma_start(vec_rows[1][k:k + 1, :], v.rearrange("(o e) -> o e", o=1)).then_inc(cols_loaded[1], 16)
                load_x(batch(0, 1))
                sp.dma_start(wv0_sb[:], wv0).then_inc(wv_loaded, 16)
                sp.dma_start(wv1_sb, wv1).then_inc(wv_loaded, 16)
                sp.dma_start(wo_sb, wo.rearrange("(c p) d -> p c d", p=P)).then_inc(wv_loaded, 16)
                for row, v, landed in ((bv0_row, bv0, rows_loaded), (gamma_row, gamma, rows_loaded),
                                       (beta_row, beta, out_free[0]), (bo_row, bo, out_free[1])):
                    sp.dma_start(row[:], v.rearrange("(o e) -> o e", o=1).broadcast_to([P, E])).then_inc(landed, 16)

            def pre1():
                pass

            def body(a, b, c, done=()):
                if b and c:
                    load_x(c, after=True)
                if a and c:
                    for g in range(GROUPS):
                        load_ctx(c, g, after=True)
                if b is None:
                    return
                dst = out[bass.ds(b.n, 1)].rearrange("o (t p) e -> p (o t) e", p=P)
                for h in range(2):
                    sp.wait_ge(o_done, 2 * b.n + h + 1)
                    sp.dma_start(dst[:, 2 * h:2 * h + 2, :], o_sb[:, 2 * h:2 * h + 2, :]
                                 ).then_inc(out_free[h], 16)

            run(body, (pre0, pre1), sp)
            for h in range(2):
                sp.wait_ge(out_free[h], 16 * (B + 1))

        @blk.tensor
        def _(pe):
            def split3(ps, w_hi, w_lo, m_hi, m_lo, start=True, stop=True):
                nc.tensor.matmul(ps, w_lo, m_hi, start=start, stop=False)
                nc.tensor.matmul(ps, w_hi, m_lo, start=False, stop=False)
                return nc.tensor.matmul(ps, w_hi, m_hi, start=False, stop=stop)

            def turn_ctx(a, g):
                pe.wait_ge(ctx_loaded[g], 16 * (a.n + 1))
                for k, i in enumerate(group(g)):
                    m = rows(i)
                    mm = nc.tensor.transpose(ps_misc[:, k * P:k * P + m], ctx_sb[0:m, i, :],
                                             ident[0:m, 0:m])
                mm.then_inc(ctxT_ps, 1)

            def turn_x(a, c):
                if c == 0:
                    pe.wait_ge(x_loaded[a.par], 16 * (a.use + 1))
                for t in range(TB):
                    mm = nc.tensor.transpose(ps_misc[:, t * P:(t + 1) * P], x_sb[a.par][:, t, c * P:(c + 1) * P],
                                             ident[:])
                mm.then_inc(xT_ps, 1)

            def project_q0(a, _):
                pe.wait_ge(xT_done, EC * (a.n + 1))
                for c in range(EC):
                    mm = nc.tensor.matmul(ps_misc[:], a_sb[:, 0, c, :], xT[:, c, :], start=(c == 0), stop=(c == EC - 1))
                mm.then_inc(qw0_ps, 1)

            def project_bias0(a, _):
                for c in range(EC):
                    mm = nc.tensor.matmul(ps_misc[:], u0_rep[:, c, :], xT[:, c, :], start=(c == 0), stop=(c == EC - 1))
                mm.then_inc(cb_ps, 1)

            def scores0(a, i):
                if i % TB == 0:
                    pe.wait_ge(ctxT_lo_done, GROUPS * a.n + i // TB + 1)
                if i == 0:
                    pe.wait_ge(qw0_lo_done, a.n + 1)
                if i >= 2 or not first(a):
                    pe.wait_ge(s0_read, MT * a.n + i - 1)
                m = slice(i * P, i * P + rows(i))
                split3(ps_s0[0:rows(i), (a.par + i) % 2, :], ctxT_hi[a.par][:, m], ctxT_lo[a.par][:, m],
                       qw0_hi[a.par][:], qw0_lo[a.par][:]).then_inc(s0_ps, 1)

            def weigh0(a, i):
                pe.wait_ge(p0_lo_done, MT * a.n + i + 1)
                if i % TB == 0:
                    pe.wait_ge(ctx_lo_done, GROUPS * a.n + i // TB + 1)
                if i == 0 and not first(a):
                    pe.wait_ge(at0_done, a.n)
                m = rows(i)
                split3(ps_acc0[:], ctx_hi[a.par][0:m, i, :], ctx_lo[a.par][0:m, i, :], p0_hi[0:m, ring0(i), :],
                       p0_lo[0:m, ring0(i), :], start=(i == 0), stop=(i == MT - 1)).then_inc(pv0_ps, 1)

            def sum_rows0(a, _):
                pe.wait_ge(wsum_done, MT * (a.n + 1))
                for t in range(TB):
                    mm = nc.tensor.matmul(ps_misc[:, t:t + 1], wsum[a.par][:, t * P:(t + 1) * P], ones[:, 0:1],
                                          start=True, stop=True)
                mm.then_inc(rowsum_ps, 1)

            def predict(a, h):
                if h == 0:
                    pe.wait_ge(at0_done, a.n + 1)
                for k in range(2):
                    t = slice((2 * h + k) * P, (2 * h + k + 1) * P)
                    mm = nc.tensor.matmul(ps_misc[:, k * E:(k + 1) * E], at0[:, t], wv0_sb[:], start=True, stop=True)
                mm.then_inc(pred_ps, 1)

            def turn_y(b, c):
                pe.wait_ge(xhat_done, TB * (b.n + 1))
                if c == 0:
                    pe.wait_ge(row1_made, MADE)
                for t in range(TB):
                    mm = nc.tensor.transpose(ps_y[c][:, t * P:(t + 1) * P], xhat[:, t, c * P:(c + 1) * P], ident[:])
                mm.then_inc(xhT_ps, 1)

            def project_q1(b, _):
                pe.wait_ge(xhT_done, EC * (b.n + 1))
                for c in range(EC):
                    mm = nc.tensor.matmul(ps_q1, a1_gamma[:, c, :], xhT[:, c, :], start=(c == 0), stop=(c == EC - 1))
                mm.then_inc(qw1_ps, 1)

            def scores1(b, i):
                t, k = i // len(chunks), i % len(chunks)
                if i == 0:
                    pe.wait_ge(qw1_lo_done, b.n + 1)
                before = t - 2 if last(b) else t - 1
                if before >= 0 and k in (0, len(chunks) - 1):
                    pe.wait_ge(exp1_done, 2 * (TB * b.n + before) + (1 if k == 0 else 2))
                q = slice(t * P, (t + 1) * P)
                lo, hi = chunks[k]
                split3(s1_banks(b, t)[:, k, 0:hi - lo], qw1_hi[:, q], qw1_lo[:, q], ctxT_hi[b.par][:, lo:hi],
                       ctxT_lo[b.par][:, lo:hi]).then_inc(s1_ps, 1)

            def turn_p1(b, i):
                if i == 0:
                    pe.wait_ge(exp1_done, 2 * TB * (b.n + 1))
                elif i >= 3:
                    pe.wait_ge(p1T_lo_done, MT * b.n + i - 2)
                m = rows(i)
                for t in range(TB):
                    mm = nc.tensor.transpose(ps_turn[i % 3][0:m, t * P:(t + 1) * P], p1[:, t, i * P:i * P + m], ident[:])
                mm.then_inc(p1T_ps, 1)

            def weigh1(b, i):
                pe.wait_ge(p1T_lo_done, MT * b.n + i + 1)
                m = rows(i)
                split3(ps_acc1, ctx_hi[b.par][0:m, i, :], ctx_lo[b.par][0:m, i, :], p1T_hi[0:m, i % RING, :],
                       p1T_lo[0:m, i % RING, :], start=(i == 0), stop=(i == MT - 1)).then_inc(pv1_ps, 1)

            def project_out(b, h):
                if h == 0:
                    pe.wait_ge(at1_done, b.n + 1)
                for k in range(2):
                    t = slice((2 * h + k) * P, (2 * h + k + 1) * P)
                    mm = nc.tensor.matmul(ps_out[h][:, k * E:(k + 1) * E], at1[:, t], w2_sb[:], start=True, stop=True)
                mm.then_inc(out_ps, 1)

            def turn_weights(n, ps_q, ps_k):
                pe.wait_ge(w_loaded[n], 16 * 2)
                for h in range(EC):
                    for c in range(EC):
                        mm = nc.tensor.transpose(ps_q[:, h * E + c * P:h * E + (c + 1) * P],
                                                 wq_sb[n][:, c, h * P:(h + 1) * P], ident[:])
                mm.then_inc(wT_turned, 1)
                for h in range(EC):
                    mm = nc.tensor.transpose(ps_k[:, h * P:(h + 1) * P], wk_sb[n][:, h * P:(h + 1) * P], ident[:])
                mm.then_inc(wT_turned, 1)

            def turn_vectors(n, ps):
                pe.wait_ge(cols_loaded[n], 16 * NV[n])
                for c in range(EC):
                    mm = nc.tensor.transpose(ps[:, c * NV[n]:(c + 1) * NV[n]], vec_rows[n][:, c * P:(c + 1) * P],
                                             ident[0:NV[n], 0:NV[n]])
                mm.then_inc(cols_turned, 1)

            def make_a(n, ps):
                for c in range(EC):
                    for h in range(EC):
                        mm = nc.tensor.matmul(ps[:, c * P:(c + 1) * P], wqT[n][:, h, c * P:(c + 1) * P],
                                              wkT[:, n, h, :], start=(h == 0), stop=(h == EC - 1))
                return mm

            def keep_warm(n):
                for _ in range(n):
                    nc.tensor.matmul(ps_s0[:, 0, 0:P], ident[:], ident[:], start=True, stop=True)

            def pre0():
                pe.wait_ge(ident_done, 1)
                keep_warm(WARM[0])
                turn_weights(0, s1_bank(0), s1_bank(1))
                turn_vectors(0, ps_acc0)
                turn_x(batch(0, 0), 0)
                keep_warm(WARM[1])
                pe.wait_ge(wT_copied, 2)
                make_a(0, s1_bank(2))
                pe.wait_ge(reps_done, EC)
                for c in range(EC):
                    for h in range(EC):
                        mm = nc.tensor.matmul(s1_bank(2)[:, E + c * P:E + (c + 1) * P], wqT[0][:, h, c * P:(c + 1) * P],
                                              bk_rep[0][:, h, :], start=(h == 0), stop=(h == EC - 1))
                mm.then_inc(made_ps, 1)
                for h in range(EC):
                    nc.tensor.matmul(ps_acc0[:, 0:1], wkT[:, 0, h, :], bq_col[0][:, h:h + 1],
                                     start=(h == 0), stop=(h == EC - 1))
                for h in range(EC):
                    mm = nc.tensor.matmul(ps_acc0[:, 1:2], bk_rep[0][:, h, :], bq_col[0][:, h:h + 1],
                                          start=(h == 0), stop=(h == EC - 1))
                mm.then_inc(small_ps, 1)
                pe.wait_ge(xT_done, 1)
                turn_x(batch(0, 0), 1)
                pe.wait_ge(xT_done, 2)
                turn_ctx(batch(0, 0), 0)
                keep_warm(WARM[2])
                pe.wait_ge(small_sb, 1)
                pe.wait_ge(made_sb, 2)
                pe.wait_ge(ctxT_lo_done, 1)

            def pre1():
                turn_weights(1, s1_bank(0), s1_bank(1))
                pe.wait_ge(wv_loaded, 16 * 3)
                for h in range(EC):
                    mm = nc.tensor.transpose(s1_bank(1)[:, E + h * P:E + (h + 1) * P], wv1_sb[:, h * P:(h + 1) * P], ident[:])
                mm.then_inc(wT_turned, 1)
                turn_vectors(1, s1_bank(3))
                pe.wait_ge(wT_copied, 5)
                make_a(1, s1_bank(2))
                pe.wait_ge(reps_done, 3 * EC)
                for h in range(EC):
                    mm = nc.tensor.matmul(s1_bank(2)[:, E:2 * E], bk_rep[1][:, h, :], wqT[1][:, h, :],
                                          start=(h == 0), stop=(h == EC - 1))
                mm.then_inc(made_ps, 1)
                for h in range(EC):
                    nc.tensor.matmul(s1_bank(3)[:, 0:E], wvT[:, h, :], wo_sb[:, h, :], start=(h == 0), stop=(h == EC - 1))
                for h in range(EC):
                    mm = nc.tensor.matmul(s1_bank(3)[:, E:2 * E], bv1_rep[:, h, :], wo_sb[:, h, :],
                                          start=(h == 0), stop=(h == EC - 1))
                mm.then_inc(made_ps, 1)
                for h in range(EC):
                    nc.tensor.matmul(s1_bank(0)[:, 1:2], bk_rep[1][:, h, :], bq_col[1][:, h:h + 1],
                                     start=(h == 0), stop=(h == EC - 1))
                for h in range(EC):
                    nc.tensor.matmul(s1_bank(0)[:, 0:1], wkT[:, 1, h, :], bq_col[1][:, h:h + 1], start=(h == 0), stop=False)
                pe.wait_ge(made_sb, 3)
                for c in range(EC):
                    mm = nc.tensor.matmul(s1_bank(0)[:, 0:1], a_sb[:, 1, c, :], beta_col[:, c:c + 1], start=False,
                                          stop=(c == EC - 1))
                mm.then_inc(small_ps, 1)

            MISC = ("turn_x", "project_q0", "project_bias0", "turn_ctx", "sum_rows0", "predict")

            def misc_read(step, a, b, c, done):
                here = [(n, {"a": a, "b": b, "c": c}[who], i) for n, who, i in TENSOR_ORDER[:step]
                        if n in MISC and (n, i) not in done]
                before = [(n, {"a": b, "c": a}[who], i) for n, who, i in TENSOR_ORDER if n in MISC]
                for n, bt, i in reversed(before + here):
                    if bt:
                        break
                else:
                    return
                if n == "turn_x":
                    pe.wait_ge(xT_done, EC * bt.n + i + 1)
                elif n == "project_q0":
                    pe.wait_ge(qw0_lo_done, bt.n + 1)
                elif n == "project_bias0":
                    pe.wait_ge(cb_done, bt.n + 1)
                elif n == "sum_rows0":
                    pe.wait_ge(rowsum_done, bt.n + 1)
                elif n == "turn_ctx":
                    pe.wait_ge(ctxT_lo_done, GROUPS * bt.n + i + 1)
                else:
                    pe.wait_ge(xr_done, 2 * bt.n + i + 1)

            steps = {f.__name__: f for f in (
                turn_x, project_q0, project_bias0, turn_ctx, scores0, weigh0, sum_rows0, predict, turn_y, project_q1, scores1, turn_p1, weigh1, project_out)}

            def body(a, b, c, done=()):
                for step, (name, who, i) in enumerate(TENSOR_ORDER):
                    bt = {"a": a, "b": b, "c": c}[who]
                    if bt and (name, i) not in done:
                        if name in MISC:
                            misc_read(step, a, b, c, done)
                        steps[name](bt, i)

            run(body, (pre0, pre1), pe)

        @blk.scalar
        def _(act):
            def ctx_high(a, g):
                act.wait_ge(ctxT_ps, GROUPS * a.n + g + 1)
                lo, hi = group_cols(g)
                nc.scalar.copy(ctxT_hi[a.par][:, lo:hi], ps_misc[:, 0:hi - lo]).then_inc(ctxT_hi_done, 1)

            def ctx_split(a, g):
                act.wait_ge(ctx_loaded[g], 16 * (a.n + 1))
                if g == 0 and not (isinstance(a.n, int) and a.n < 2):
                    act.wait_ge(pv1_ps, MT * (a.n - 2) + group(g)[-1] + 1)
                m = rows(group(g)[0])
                tiles = slice(group(g)[0], group(g)[-1] + 1)
                nc.scalar.copy(ctx_hi[a.par][0:m, tiles, :], ctx_sb[0:m, tiles, :]).then_inc(ctx_hi_done, 1)

            def x_turned(a, c):
                act.wait_ge(xT_ps, EC * a.n + c + 1)
                if c == 0 and not first(a):
                    act.wait_ge(cb_ps, a.n)
                nc.scalar.copy(xT[:, c, :], ps_misc[:]).then_inc(xT_done, 1)

            def q0_high(a, _):
                act.wait_ge(qw0_ps, a.n + 1)
                nc.scalar.activation(qw0_hi[a.par][:], ps_misc[:], ACT.Identity, bias=qb0, scale=1.0
                                     ).then_inc(qw0_hi_done, 1)

            def bias0(a, _):
                act.wait_ge(cb_ps, a.n + 1)
                nc.scalar.activation(cb[a.par][:], ps_misc[:], ACT.Identity, bias=bqbk0, scale=1.0
                                     ).then_inc(cb_done, 1)

            def exp0(a, i):
                act.wait_ge(s0_read, MT * a.n + i + 1)
                if (n := before0(a, i)) is not None:
                    act.wait_ge(p0_lo_done, n)
                m = rows(i)
                nc.scalar.activation(p0[0:m, ring0(i), :], s0_sb[0:m, (a.par + i) % 2, :], ACT.Exp, bias=min0[0:m, i:i + 1],
                                     scale=-1.0, accum_out=sum0[0:m, i:i + 1]).then_inc(exp0_done, 1)

            def p0_high(a, i):
                act.wait_ge(r0_done, MT * a.n + i + 1)
                if (n := before0(a, i)) is not None:
                    act.wait_ge(pv0_ps, n)
                    act.wait_ge(wsum_done, n)
                m = rows(i)
                nc.scalar.activation(p0_hi[0:m, ring0(i), :], p0[0:m, ring0(i), :], ACT.Copy, scale=r0[0:m, i:i + 1]
                                     ).then_inc(p0_hi_done, 1)

            def weighed0(a, _):
                act.wait_ge(pv0_ps, MT * (a.n + 1))
                if not first(a):
                    act.wait_ge(pred_ps, 2 * a.n)
                nc.scalar.copy(at0[:], ps_acc0[:]).then_inc(at0_done, 1)

            def y_turned(b, c):
                act.wait_ge(xhT_ps, EC * b.n + c + 1)
                if c == 0:
                    act.wait_ge(row1_made, MADE)
                nc.scalar.copy(xhT[:, c, :], ps_y[c]).then_inc(xhT_done, 1)

            def q1_high(b, _):
                act.wait_ge(qw1_ps, b.n + 1)
                nc.scalar.activation(qw1_hi[:], ps_q1, ACT.Identity, bias=scaled1[:, 0:1], scale=1.0
                                     ).then_inc(qw1_hi_done, 1)

            def exp1(b, i):
                t, h = i // 2, i % 2
                if h == 0:
                    act.wait_ge(bias1_done, TB * b.n + t + 1)
                if h == 0:
                    scores = s1_banks(b, t)[:, 0:len(chunks) - 1, 0:CHUNK]
                    exps = p1[:, t, 0:last_lo].rearrange("p (k m) -> p k m", m=CHUNK)
                else:
                    scores, exps = s1_banks(b, t)[:, len(chunks) - 1, 0:M - last_lo], p1[:, t, last_lo:M]
                nc.scalar.activation(exps, scores, ACT.Exp, bias=bias1[:, t:t + 1], scale=1.0,
                                     accum_out=sum1[:, h, t:t + 1]).then_inc(exp1_done, 1)

            def p1_turned(b, i):
                act.wait_ge(p1T_ps, MT * b.n + i + 1)
                if i >= RING:
                    act.wait_ge(pv1_ps, MT * b.n + i + 1 - RING)
                m = rows(i)
                nc.scalar.copy(p1T_hi[0:m, i % RING, :], ps_turn[i % 3][0:m, :]).then_inc(p1T_hi_done, 1)

            def weighed1(b, _):
                act.wait_ge(pv1_ps, MT * (b.n + 1))
                nc.scalar.copy(at1[:], ps_acc1).then_inc(at1_done, 1)

            def pre0():
                for k, v in enumerate((bq0, bk0)):
                    act.dma_start(vec_rows[0][k:k + 1, :], v.rearrange("(o e) -> o e", o=1)).then_inc(cols_loaded[0], 16)
                act.wait_ge(wT_turned, 1)
                nc.scalar.copy(wqT[0].rearrange("p h e -> p (h e)"), s1_bank(0)).then_inc(wT_copied, 1)
                act.wait_ge(wT_turned, 2)
                nc.scalar.copy(wkT[:, 0].rearrange("p h l -> p (h l)"), s1_bank(1)[:, 0:E]).then_inc(wT_copied, 1)
                x_turned(batch(0, 0), 0)
                act.wait_ge(made_ps, 1)
                nc.scalar.copy(a_sb[:, 0].rearrange("p c l -> p (c l)"), s1_bank(2)[:, 0:E]).then_inc(made_sb, 1)
                nc.scalar.copy(u0_rep[:].rearrange("p c l -> p (c l)"), s1_bank(2)[:, E:2 * E]).then_inc(made_sb, 1)
                x_turned(batch(0, 0), 1)
                act.wait_ge(small_ps, 1)
                nc.scalar.copy(small[0][:], ps_acc0[:, 0:2]).then_inc(small_sb, 1)
                ctx_high(batch(0, 0), 0)
                act.wait_ge(small_sb, 1)

            def pre1():
                act.wait_ge(wT_turned, 3)
                nc.scalar.copy(wqT[1].rearrange("p h e -> p (h e)"), s1_bank(0)).then_inc(wT_copied, 1)
                act.wait_ge(wT_turned, 5)
                nc.scalar.copy(wkT[:, 1].rearrange("p h l -> p (h l)"), s1_bank(1)[:, 0:E]).then_inc(wT_copied, 1)
                nc.scalar.copy(wvT.rearrange("p h l -> p (h l)"), s1_bank(1)[:, E:2 * E]).then_inc(wT_copied, 1)
                act.wait_ge(made_ps, 2)
                nc.scalar.copy(a_sb[:, 1].rearrange("p c l -> p (c l)"), s1_bank(2)[:, 0:E]).then_inc(made_sb, 1)
                nc.scalar.copy(u1_row[:], s1_bank(2)[:, E:2 * E]).then_inc(made_sb, 1)
                act.wait_ge(made_ps, 3)
                nc.scalar.copy(w2_sb[:], s1_bank(3)[:, 0:E]).then_inc(made_sb, 1)
                act.wait_ge(small_ps, 2)
                nc.scalar.copy(small[1][:], s1_bank(0)[:, 0:2]).then_inc(small_sb, 1)

            steps = {f.__name__: f for f in (
                x_turned, q0_high, bias0, ctx_high, ctx_split, exp0, p0_high, weighed0, y_turned, q1_high, exp1, p1_turned, weighed1)}

            def body(a, b, c, done=()):
                for name, who, i in SCALAR_ORDER:
                    bt = {"a": a, "b": b, "c": c}[who]
                    if bt and (name, i) not in done:
                        steps[name](bt, i)

            run(body, (pre0, pre1), act)

        @blk.vector
        def _(dve):
            def ctxT_low(a, g):
                dve.wait_ge(ctxT_hi_done, GROUPS * a.n + g + 1)
                lo, hi = group_cols(g)
                nc.vector.tensor_tensor(ctxT_lo[a.par][:, lo:hi], ps_misc[:, 0:hi - lo],
                                        ctxT_hi[a.par][:, lo:hi].bitcast(F32), ALU.subtract).then_inc(ctxT_lo_done, 1)

            def q0_low(a, _):
                dve.wait_ge(qw0_hi_done, a.n + 1)
                nc.vector.scalar_tensor_tensor(qw0_lo[a.par][:], ps_misc[:], qb0, qw0_hi[a.par][:].bitcast(F32),
                                               ALU.add, ALU.subtract).then_inc(qw0_lo_done, 1)

            def max0(a, i):
                if i == 0:
                    dve.wait_ge(cb_done, a.n + 1)
                if i >= 2 or not first(a):
                    dve.wait_ge(exp0_done, MT * a.n + i - 1)
                wait_apart(dve, s0_ps, MT * a.n + i + 1)
                m = rows(i)
                nc.vector.tensor_tensor_reduce(out=s0_sb[0:m, (a.par + i) % 2, :], in0=ps_s0[0:m, (a.par + i) % 2, :], in1=cb[a.par][0:m, :],
                                               scale=-SCALE, scalar=BIG, op0=ALU.add, op1=ALU.min,
                                               accum_out=min0[0:m, i:i + 1]).then_inc(s0_read, 1)

            def recip0(a, i):
                dve.wait_ge(exp0_done, MT * a.n + i + 1)
                m = rows(i)
                nc.vector.reciprocal(r0[0:m, i:i + 1], sum0[0:m, i:i + 1]).then_inc(r0_done, 1)

            def p0_low(a, i):
                dve.wait_ge(p0_hi_done, MT * a.n + i + 1)
                m = rows(i)
                nc.vector.scalar_tensor_tensor(p0_lo[0:m, ring0(i), :], p0[0:m, ring0(i), :], r0[0:m, i:i + 1],
                                               p0_hi[0:m, ring0(i), :].bitcast(F32), ALU.mult, ALU.subtract
                                               ).then_inc(p0_lo_done, 1)

            def p1_low(b, i):
                dve.wait_ge(p1T_hi_done, MT * b.n + i + 1)
                m = rows(i)
                nc.vector.tensor_tensor(p1T_lo[0:m, i % RING, :], ps_turn[i % 3][0:m, :],
                                        p1T_hi[0:m, i % RING, :].bitcast(F32), ALU.subtract).then_inc(p1T_lo_done, 1)

            def bias_x0(a, _):
                dve.wait_ge(rowsum_ps, a.n + 1)
                nc.vector.tensor_copy(rowsum0[:], ps_misc[:, 0:TB]).then_inc(rowsum_done, 1)
                if first(a):
                    dve.wait_ge(rows_loaded, 16 * 2)
                dve.wait_ge(x_loaded[a.par], 16 * (a.use + 1))
                dve.wait_ge(rowsum_done, a.n + 1)
                for t in range(TB):
                    ins = nc.vector.scalar_tensor_tensor(xr[:, t, :], bv0_row[:], rowsum0[:, t:t + 1], x_sb[a.par][:, t, :],
                                                         ALU.mult, ALU.add)
                ins.then_inc(xbias_done, 1)

            def residual0(a, h):
                two = slice(2 * h, 2 * h + 2)
                if h == 0:
                    dve.wait_ge(xbias_done, a.n + 1)
                dve.wait_ge(pred_ps, 2 * a.n + h + 1)
                nc.vector.tensor_tensor(xr[:, two, :], ps_misc[:].rearrange("p (t e) -> p t e", e=E),
                                        xr[:, two, :], ALU.add).then_inc(xr_done, 1)

            def moments0(a, h):
                two = slice(2 * h, 2 * h + 2)
                dve.wait_ge(xr_done, 2 * a.n + h + 1)
                for t in (2 * h, 2 * h + 1):
                    nc.vector.bn_stats(stats[:, t, :], xr[:, t, :]).then_inc(stats_done, 1)
                for t in (2 * h, 2 * h + 1):
                    wait_apart(dve, stats_done, TB * a.n + t + 1)
                    nc.vector.bn_aggr(mv[:, t, :], stats[:, t, :]).then_inc(mv_done, 1)
                dve.wait_ge(mv_done, TB * a.n + 2 * h + 2)
                nc.vector.tensor_scalar(var_eps[:, two, :], mv[:, two, 1:2], LN_EPS, None, ALU.add).then_inc(var_done, 1)

            def normalised(a, h):
                dve.wait_ge(rstd_done, 2 * a.n + h + 1)
                if h == 0 and not first(a):
                    dve.wait_ge(xhT_ps, EC * a.n)
                    dve.wait_ge(y_part_done, a.n)
                for t in (2 * h, 2 * h + 1):
                    nc.vector.tensor_scalar(xhat[:, t, :], xr[:, t, :], mv[:, t, 0:1], rstd[:, t, :], ALU.subtract,
                                            ALU.mult).then_inc(xhat_done, 1)

            def bias_row1(b, _):
                dve.wait_ge(row1_made, MADE)
                dve.wait_ge(xhat_done, TB * (b.n + 1))
                for t in range(TB):
                    nc.vector.tensor_tensor_reduce(out=junk[:, t, :], in0=xhat[:, t, :], in1=u1_gamma[:], scale=1.0,
                                                   scalar=c1_const[:, 0:1], op0=ALU.mult, op1=ALU.add,
                                                   accum_out=c1[:, t:t + 1]).then_inc(c1_done, 1)

            def q1_low(b, _):
                dve.wait_ge(qw1_hi_done, b.n + 1)
                nc.vector.scalar_tensor_tensor(qw1_lo[:], ps_q1, scaled1[:, 0:1], qw1_hi[:].bitcast(F32), ALU.add,
                                               ALU.subtract).then_inc(qw1_lo_done, 1)

            def rowmax1(b, i):
                t, k = i // len(chunks), i % len(chunks)
                lo, hi = chunks[k]
                dve.wait_ge(s1_ps, len(chunks) * TB * b.n + i + 1)
                nc.vector.tensor_reduce(max1[:, t, k:k + 1], s1_banks(b, t)[:, k, 0:min(hi, M) - lo], AX_X, ALU.max
                                        ).then_inc(max1_done, 1)

            def bias1_of(b, t):
                if t == 0:
                    dve.wait_ge(c1_done, TB * (b.n + 1))
                dve.wait_ge(max1_done, len(chunks) * (TB * b.n + t + 1))
                nc.vector.tensor_reduce(neg_max1[:, t:t + 1], max1[:, t, :], AX_X, ALU.max, negate=True
                                        ).then_inc(neg_max1_done, 1)
                dve.wait_ge(neg_max1_done, TB * b.n + t + 1)
                nc.vector.scalar_tensor_tensor(bias1[:, t:t + 1], neg_max1[:, t:t + 1], c1[:, t:t + 1], c1[:, t:t + 1],
                                               ALU.subtract, ALU.add).then_inc(bias1_done, 1)

            def recip1(b, _):
                dve.wait_ge(exp1_done, 2 * TB * (b.n + 1))
                nc.vector.tensor_tensor(sum1_all[:], sum1[:, 0, :], sum1[:, 1, :], ALU.add).then_inc(sum1_done, 1)
                dve.wait_ge(sum1_done, b.n + 1)
                nc.vector.reciprocal(r1[:], sum1_all[:]).then_inc(r1_done, 1)

            def finish(b, h):
                if h == 0:
                    dve.wait_ge(r1_done, b.n + 1)
                    dve.wait_ge(y_res_done, b.n + 1)
                dve.wait_ge(out_free[h], 16 * (b.n + 1))
                dve.wait_ge(out_ps, 2 * b.n + h + 1)
                for k in range(2):
                    t = 2 * h + k
                    ins = nc.vector.scalar_tensor_tensor(o_sb[:, t, :], ps_out[h][:, k * E:(k + 1) * E], r1[:, t:t + 1],
                                                         y_res[:, t, :], ALU.mult, ALU.add)
                ins.then_inc(o_done, 1)

            def repeat(n, ps, reps):
                dve.wait_ge(cols_turned, n + 1)
                nc.vector.tensor_copy(cols[n][:].rearrange("p c n -> p (c n)"), ps[:, 0:EC * NV[n]]).then_inc(cols_done, 1)
                dve.wait_ge(cols_done, n + 1)
                for rep, col in reps:
                    for h in range(EC):
                        nc.vector.tensor_scalar(rep[:, h, :], ones[:], col[:, h:h + 1], None, ALU.mult
                                                ).then_inc(reps_done, 1)

            def pre0():
                for p in range(2):
                    nc.vector.memset(ctxT_hi[p][:, M:MPAD].bitcast(F32), 0.0)
                    nc.vector.memset(ctxT_lo[p][:, M:MPAD].bitcast(F32), 0.0)
                nc.vector.memset(ones[:], 1.0).then_inc(ones_done, 1)
                dve.wait_ge(ones_done, 1)
                repeat(0, ps_acc0, ((bk_rep[0], bk_col[0]),))
                ctxT_low(batch(0, 0), 0)
                dve.wait_ge(small_sb, 1)

            def pre1():
                repeat(1, s1_bank(3), ((bk_rep[1], bk_col[1]), (bv1_rep, bv1_col)))
                dve.wait_ge(rows_loaded, 16 * 2)
                for h in range(2):
                    dve.wait_ge(out_free[h], 16)
                nc.vector.tensor_tensor(betaob_part[:], beta_row[:], bo_row[:], ALU.add).then_inc(row1_made, 1)
                dve.wait_ge(made_sb, 4)
                for c in range(EC):
                    nc.vector.tensor_scalar(a1_gamma[:, c, :], a_sb[:, 1, c, :], gamma_col[:, c:c + 1], SCALE, ALU.mult, ALU.mult
                                            ).then_inc(row1_made, 1)
                nc.vector.scalar_tensor_tensor(u1_gamma[:], u1_row[:], SCALE, gamma_row[:], ALU.mult, ALU.mult
                                               ).then_inc(row1_made, 1)
                dve.wait_ge(made_sb, 5)
                dve.wait_ge(row1_made, 1)
                nc.vector.tensor_tensor(betaob_row[:], s1_bank(3)[:, E:2 * E], betaob_part[:], ALU.add).then_inc(row1_made, 1)
                dve.wait_ge(small_sb, 2)
                nc.vector.tensor_scalar(scaled1[:], small[1][:], SCALE, None, ALU.mult).then_inc(row1_made, 1)
                dve.wait_ge(row1_made, MADE - 1)
                nc.vector.tensor_tensor_reduce(out=junk[:, 0, :], in0=u1_row[:], in1=beta_row[:], scale=SCALE,
                                               scalar=scaled1[:, 1:2], op0=ALU.mult, op1=ALU.add,
                                               accum_out=c1_const[:, 0:1]).then_inc(row1_made, 1)

            steps = {f.__name__: f for f in (
                ctxT_low, bias_x0, q0_low, max0, recip0, p0_low, residual0, moments0, normalised, bias_row1, q1_low, rowmax1, bias1_of, recip1, p1_low, finish)}

            def body(a, b, c, done=()):
                for name, who, i in VECTOR_ORDER:
                    bt = {"a": a, "b": b, "c": c}[who]
                    if bt and (name, i) not in done:
                        steps[name](bt, i)

            run(body, (pre0, pre1), dve)

        @blk.gpsimd
        def _(pool):
            def ctx_low(a, g):
                pool.wait_ge(ctx_hi_done, GROUPS * a.n + g + 1)
                m = rows(group(g)[0])
                tiles = slice(group(g)[0], group(g)[-1] + 1)
                nc.gpsimd.tensor_tensor(ctx_lo[a.par][0:m, tiles, :], ctx_sb[0:m, tiles, :],
                                        ctx_hi[a.par][0:m, tiles, :].bitcast(F32), ALU.subtract).then_inc(ctx_lo_done, 1)

            def sum_weights(a, i):
                pool.wait_ge(p0_lo_done, MT * a.n + i + 1)
                m = rows(i)
                total = wsum[a.par][0:m, :]
                hi, lo = (part[0:m, ring0(i), :].bitcast(F32) for part in (p0_hi, p0_lo))
                if i == 0:
                    nc.gpsimd.tensor_tensor(total, hi, lo, ALU.add).then_inc(wsum_done, 1)
                else:
                    pool.wait_ge(wsum_done, MT * a.n + i)
                    nc.gpsimd.tensor_tensor(total, total, lo, ALU.add).then_inc(wsum_part, 1)
                    pool.wait_ge(wsum_part, (MT - 1) * a.n + i)
                    nc.gpsimd.tensor_tensor(total, total, hi, ALU.add).then_inc(wsum_done, 1)

            def residual1(b, _):
                pool.wait_ge(row1_made, MADE)
                pool.wait_ge(xhat_done, TB * (b.n + 1))
                pool.wait_ge(c1_done, TB * (b.n + 1))
                for t in range(TB):
                    ins = nc.gpsimd.tensor_tensor(y_res[:, t, :], xhat[:, t, :], gamma_row[:], ALU.mult)
                ins.then_inc(y_part_done, 1)
                pool.wait_ge(y_part_done, b.n + 1)
                for t in range(TB):
                    ins = nc.gpsimd.tensor_tensor(y_res[:, t, :], y_res[:, t, :], betaob_row[:], ALU.add)
                ins.then_inc(y_res_done, 1)

            def rsqrt_var(a, h):
                pool.wait_ge(var_done, 2 * a.n + h + 1)
                two = slice(2 * h, 2 * h + 2)
                nc.gpsimd.tensor_tensor(rstd[:, two, :], var_eps[:, two, :], neg_half[:], ALU.pow).then_inc(rstd_done, 1)

            def pre0():
                nc.gpsimd.memset(neg_half[:], -0.5)
                nc.gpsimd.memset(ident[:], 0.0).then_inc(ident_zero, 1)
                pool.wait_ge(ident_zero, 1)
                nc.gpsimd.affine_select(out=ident[:], in_=ident[:], compare_op=ALU.not_equal, fill=1.0, base=0,
                                        pattern=[[-1, P]], channel_multiplier=1).then_inc(ident_done, 1)

            def pre1():
                pass

            steps = {f.__name__: f for f in (
                ctx_low, sum_weights, rsqrt_var, residual1)}

            def body(a, b, c, done=()):
                for name, who, i in GPSIMD_ORDER:
                    bt = {"a": a, "b": b, "c": c}[who]
                    if bt and (name, i) not in done:
                        steps[name](bt, i)

            run(body, (pre0, pre1), pool)


_INS = ["x", "ctx_512"] + [f"L0_xattn_{n}" for n in ("Wq", "bq", "Wk", "bk", "Wv", "bv", "gamma", "beta")] + [
    f"L1_xattn_{n}" for n in ("Wq", "bq", "Wk", "bk", "Wv", "bv", "Wo", "bo")]


def kernel(**inputs):
    import numpy as np
    import concourse.bacc as bacc
    from concourse.bass_utils import run_bass_kernel_spmd

    nc = bacc.Bacc("TRN2", target_bir_lowering=False, num_devices=1)
    arrays, args = {}, []
    for name in _INS:
        a = np.ascontiguousarray(inputs[name])
        arrays[f"in_{name}_dram"] = a
        args.append(nc.dram_tensor(f"in_{name}_dram", a.shape, mybir.dt.from_np(a.dtype), kind="ExternalInput").ap())
    shape = inputs["x"].shape
    args.append(nc.dram_tensor("out_dram", shape, F32, kind="ExternalOutput").ap())
    xattn_kernel(nc, *args)
    r = run_bass_kernel_spmd(nc, [arrays], core_ids=[0])
    return r.results[0]["out_dram"]
```

```python
from collections import namedtuple
from contextlib import ExitStack

import concourse.bass as bass
from concourse import mybir

ALU = mybir.AluOpType
ACT = mybir.ActivationFunctionType
F32 = mybir.dt.float32
F32R = mybir.dt.float32r
AX_X = mybir.AxisListType.X

P = 128
BANK = 512
LN_EPS = 1e-6
BIG = 3.0e38

TENSOR_ORDER = (
    ("project_q1", "b", 0), ("weigh0", "a", 2), ("scores1", "b", 0), ("scores1", "b", 1), ("scores1", "b", 2),
    ("scores1", "b", 3), ("turn_x", "c", 0), ("weigh0", "a", 3), ("scores0", "a", 7), ("scores0", "a", 8),
    ("turn_x", "c", 1), ("scores1", "b", 4), ("scores1", "b", 5), ("scores1", "b", 6), ("scores1", "b", 7),
    ("scores0", "a", 9), ("weigh0", "a", 4), ("project_q0", "c", 0), ("scores1", "b", 8), ("scores1", "b", 9),
    ("scores1", "b", 10), ("scores1", "b", 11), ("weigh0", "a", 5), ("weigh0", "a", 6), ("scores0", "a", 10),
    ("turn_ctx", "a", 3), ("scores1", "b", 12), ("scores1", "b", 13), ("scores1", "b", 14), ("scores1", "b", 15),
    ("weigh0", "a", 7), ("weigh0", "a", 8), ("project_bias0", "c", 0), ("scores0", "a", 11), ("turn_p1", "b", 0),
    ("turn_ctx", "c", 0), ("turn_p1", "b", 1), ("turn_p1", "b", 2), ("weigh0", "a", 9), ("scores0", "a", 12),
    ("scores0", "c", 0), ("weigh1", "b", 0), ("turn_p1", "b", 3), ("turn_p1", "b", 4), ("weigh1", "b", 1),
    ("turn_p1", "b", 5), ("scores0", "c", 1), ("turn_ctx", "c", 1), ("weigh1", "b", 2), ("turn_p1", "b", 6),
    ("weigh0", "a", 10), ("turn_p1", "b", 7), ("weigh1", "b", 3), ("turn_p1", "b", 8), ("scores0", "c", 2),
    ("weigh1", "b", 4), ("turn_p1", "b", 9), ("weigh1", "b", 5), ("weigh0", "a", 11), ("weigh1", "b", 6),
    ("sum_rows0", "a", 0), ("weigh0", "a", 12), ("scores0", "c", 3), ("weigh1", "b", 7), ("turn_p1", "b", 10),
    ("turn_p1", "b", 11), ("weigh1", "b", 8), ("predict", "a", 0), ("weigh0", "c", 0), ("turn_p1", "b", 12),
    ("weigh1", "b", 9), ("predict", "a", 1), ("weigh1", "b", 10), ("scores0", "c", 4), ("weigh1", "b", 11),
    ("scores0", "c", 5), ("weigh1", "b", 12), ("weigh0", "c", 1), ("turn_ctx", "c", 2), ("project_out", "b", 0),
    ("project_out", "b", 1), ("turn_y", "a", 0), ("turn_y", "a", 1), ("scores0", "c", 6),
)
SCALAR_ORDER = (
    ("load_x", "c", 0), ("p0_high", "a", 5), ("q1_high", "b", 0), ("exp0", "a", 6), ("x_turned", "c", 0),
    ("p0_high", "a", 6), ("exp1", "b", 0), ("exp0", "a", 7), ("exp1", "b", 1), ("x_turned", "c", 1),
    ("p0_high", "a", 7), ("exp0", "a", 8), ("exp1", "b", 2), ("p0_high", "a", 8), ("exp1", "b", 3), ("exp0", "a", 9),
    ("q0_high", "c", 0), ("exp1", "b", 4), ("exp1", "b", 5), ("ctx_high", "a", 3), ("p0_high", "a", 9),
    ("exp1", "b", 6), ("exp1", "b", 7), ("bias0", "c", 0), ("exp0", "a", 10), ("ctx_high", "c", 0),
    ("p1_turned", "b", 0), ("p1_turned", "b", 1), ("p0_high", "a", 10), ("exp0", "a", 11), ("p1_turned", "b", 2),
    ("p0_high", "a", 11), ("p1_turned", "b", 3), ("exp0", "a", 12), ("ctx_split", "a", 3), ("p1_turned", "b", 4),
    ("p1_turned", "b", 5), ("exp0", "c", 0), ("ctx_high", "c", 1), ("p1_turned", "b", 6), ("p0_high", "a", 12),
    ("p0_high", "c", 0), ("p1_turned", "b", 7), ("exp0", "c", 1), ("ctx_split", "c", 0), ("p0_high", "c", 1),
    ("exp0", "c", 2), ("p1_turned", "b", 8), ("p1_turned", "b", 9), ("weighed0", "a", 0), ("p0_high", "c", 2),
    ("p1_turned", "b", 10), ("exp0", "c", 3), ("p1_turned", "b", 11), ("p1_turned", "b", 12), ("p0_high", "c", 3),
    ("exp0", "c", 4), ("weighed1", "b", 0), ("ctx_split", "c", 1), ("ctx_split", "c", 2), ("p0_high", "c", 4),
    ("exp0", "c", 5), ("y_turned", "a", 0), ("y_turned", "a", 1), ("ctx_high", "c", 2),
)
VECTOR_ORDER = (
    ("q1_low", "b", 0), ("max0", "a", 6), ("p0_low", "a", 5), ("rowmax1", "b", 0), ("rowmax1", "b", 1),
    ("rowmax1", "b", 2), ("rowmax1", "b", 3), ("recip0", "a", 6), ("bias1_of", "b", 0), ("xT_low", "c", 0),
    ("max0", "a", 7), ("max0", "a", 8), ("p0_low", "a", 6), ("rowmax1", "b", 4), ("recip0", "a", 7),
    ("rowmax1", "b", 5), ("rowmax1", "b", 6), ("rowmax1", "b", 7), ("xT_low", "c", 1), ("bias1_of", "b", 1),
    ("max0", "a", 9), ("recip0", "a", 8), ("p0_low", "a", 7), ("rowmax1", "b", 8), ("rowmax1", "b", 9),
    ("rowmax1", "b", 10), ("rowmax1", "b", 11), ("recip0", "a", 9), ("bias1_of", "b", 2), ("q0_low", "c", 0),
    ("p0_low", "a", 8), ("rowmax1", "b", 12), ("rowmax1", "b", 13), ("rowmax1", "b", 14), ("rowmax1", "b", 15),
    ("ctxT_low", "a", 3), ("bias1_of", "b", 3), ("max0", "a", 10), ("p0_low", "a", 9), ("max0", "a", 11),
    ("recip0", "a", 10), ("ctxT_low", "c", 0), ("p1_low", "b", 0), ("p1_low", "b", 1), ("p0_low", "a", 10),
    ("recip0", "a", 11), ("max0", "a", 12), ("p1_low", "b", 2), ("max0", "c", 0), ("p0_low", "a", 11),
    ("p1_low", "b", 3), ("p1_low", "b", 4), ("recip0", "a", 12), ("max0", "c", 1), ("recip0", "c", 0),
    ("p1_low", "b", 5), ("p1_low", "b", 6), ("p0_low", "a", 12), ("p0_low", "c", 0), ("p1_low", "b", 7),
    ("recip0", "c", 1), ("max0", "c", 2), ("recip1", "b", 0), ("ctxT_low", "c", 1), ("p0_low", "c", 1),
    ("recip0", "c", 2), ("p1_low", "b", 8), ("p1_low", "b", 9), ("bias_x0", "a", 0), ("at0_low", "a", 0),
    ("max0", "c", 3), ("p0_low", "c", 2), ("p1_low", "b", 10), ("residual0", "a", 0), ("recip0", "c", 3),
    ("p1_low", "b", 11), ("moments0", "a", 0), ("p1_low", "b", 12), ("residual0", "a", 1), ("max0", "c", 4),
    ("moments0", "a", 1), ("max0", "c", 5), ("recip0", "c", 4), ("normalised", "a", 0), ("normalised", "a", 1),
    ("p0_low", "c", 3), ("p0_low", "c", 4), ("finish", "b", 0), ("recip0", "c", 5), ("finish", "b", 1),
    ("bias_row1", "a", 0), ("ctxT_low", "c", 2),
)
GPSIMD_ORDER = (
    ("sum_weights", "a", 3), ("ctx_low", "a", 2), ("residual1", "b", 0), ("sum_weights", "a", 4),
    ("sum_weights", "a", 5), ("sum_weights", "a", 6), ("sum_weights", "a", 7), ("sum_weights", "a", 8),
    ("sum_weights", "a", 9), ("sum_weights", "a", 10), ("sum_weights", "a", 11), ("sum_weights", "a", 12),
    ("ctx_low", "a", 3), ("sum_weights", "c", 0), ("ctx_low", "c", 0), ("sum_weights", "c", 1),
    ("sum_weights", "c", 2), ("rsqrt_var", "a", 0), ("rsqrt_var", "a", 1), ("ctx_low", "c", 1),
)
WARM = (10, 2, 4)

Batch = namedtuple("Batch", "n use par")


def batch(pair, k):
    return Batch(2 * pair + k, pair + k // 2, k % 2)


def first(bt):
    return isinstance(bt.n, int) and bt.n == 0


def xattn_kernel(nc, x, ctx, wq0, bq0, wk0, bk0, wv0, bv0, gamma, beta,
                 wq1, bq1, wk1, bk1, wv1, bv1, wo, bo, out):
    B, T, E = x.shape
    _, M, L = ctx.shape
    TB = T // P
    EC = E // P
    MT = -(-M // P)
    MPAD = M + M % 2
    GROUPS = -(-MT // TB)
    SCALE = float(E) ** -0.5
    RING = 4

    def ring0(i):
        return 4 if i == MT - 1 else i % 4

    def before0(a, i):
        last = i - 4 if 4 <= i < MT - 1 else (i + 8 - MT if i < 4 else -1)
        if last < 0 and isinstance(a.n, int) and a.n == 0:
            return None
        return MT * a.n + last + 1

    PAIRS = (B - 2) // 2
    assert L == P and T == BANK and EC == 2 and TB == 4 and B % 2 == 0

    def rows(i):
        return min(P, M - i * P)

    def group(g):
        return range(TB * g, min(TB * g + TB, MT))

    def group_cols(g):
        return TB * g * P, min(M, TB * (g + 1) * P)

    CHUNK = -(-MPAD // 8) * 2
    chunks = [(c, min(MPAD, c + CHUNK)) for c in range(0, MPAD, CHUNK)]
    last_lo = chunks[-1][0]
    assert CHUNK <= BANK and len(chunks) == 4

    def last(bt):
        return isinstance(bt.n, int) and bt.n == B - 1

    with ExitStack() as stack:
        def sb(name, shape, dt=F32):
            return stack.enter_context(nc.sbuf_tensor(name, shape, dt))

        def sem(name):
            return stack.enter_context(nc.semaphore(name))

        p1 = sb("p1", [P, TB, M])
        p1_flat = p1[:].rearrange("p t m -> p (t m)")
        room = [0]

        def early(n):
            room[0] += n
            return p1_flat[:, room[0] - n:room[0]]

        ident = sb("ident", [P, P])
        ones = sb("ones", [P, P])
        wq_sb = [early(EC * E).rearrange("p (c h) -> p c h", c=EC) for _ in range(2)]
        wk_sb = [early(E) for _ in range(2)]
        wv0_sb = early(E)
        wv1_sb = early(E)
        wo_sb = early(EC * E).rearrange("p (c d) -> p c d", c=EC)
        NV = [2, 5]
        vec_rows = [early(E)[0:NV[0], :], sb("vec_rows1", [NV[1], E])]
        cols = [sb(f"cols{n}", [P, EC, NV[n]]) for n in range(2)]
        bq_col = [cols[n][:, :, 0] for n in range(2)]
        bk_col = [cols[n][:, :, 1] for n in range(2)]
        bv1_col, gamma_col, beta_col = cols[1][:, :, 2], cols[1][:, :, 3], cols[1][:, :, 4]
        bv0_row = sb("bv0_row", [P, E])
        gamma_row = sb("gamma_row", [P, E])
        beta_row = early(E)
        bo_row = early(E)
        wqT = [early(EC * E).rearrange("p (h e) -> p h e", h=EC) for _ in range(2)]
        wkT = early(2 * EC * P).rearrange("p (n h l) -> p n h l", n=2, h=EC)
        wvT = early(EC * P).rearrange("p (h l) -> p h l", h=EC)
        bk_rep = [early(EC * P).rearrange("p (h l) -> p h l", h=EC) for _ in range(2)]
        bv1_rep = early(EC * P).rearrange("p (h l) -> p h l", h=EC)
        a0_hi, a0_lo = (sb(f"a0_{part}", [P, EC, P], F32R) for part in ("hi", "lo"))
        a1_sb = sb("a1_sb", [P, EC, P])
        a1_gamma = sb("a1_gamma", [P, EC, P])
        u0_hi, u0_lo = (sb(f"u0_{part}", [P, EC, P], F32R) for part in ("hi", "lo"))
        wv0_hi, wv0_lo = (sb(f"wv0_{part}", [P, E], F32R) for part in ("hi", "lo"))
        u1_row = early(E)
        u1_gamma = sb("u1_gamma", [P, E])
        w2_sb = sb("w2_sb", [P, E])
        betaob_row = sb("betaob_row", [P, E])
        betaob_part = early(E)
        small = [sb(f"small{n}", [P, 2]) for n in range(2)]
        qb0 = small[0][:, 0:1]
        bqbk0 = small[0][:, 1:2]
        MADE = 7
        scaled1 = sb("scaled1", [P, 2])
        c1_const = sb("c1_const", [P, 1])

        x_sb = [sb(f"x_sb{p}", [P, TB, E]) for p in range(2)]
        ctx_sb = sb("ctx_sb", [P, MT, L])
        ctx_hi = [sb(f"ctx_hi{p}", [P, MT, L], F32R) for p in range(2)]
        ctx_lo = [sb(f"ctx_lo{p}", [P, MT, L], F32R) for p in range(2)]
        ctxT_hi = [sb(f"ctxT_hi{p}", [P, MPAD], F32R) for p in range(2)]
        ctxT_lo = [sb(f"ctxT_lo{p}", [P, MPAD], F32R) for p in range(2)]
        xT_hi, xT_lo = (sb(f"xT_{part}", [P, EC, T], F32R) for part in ("hi", "lo"))
        qw0_hi = [sb(f"qw0_hi{p}", [P, T], F32R) for p in range(2)]
        qw0_lo = [sb(f"qw0_lo{p}", [P, T], F32R) for p in range(2)]
        cb = [sb(f"cb{p}", [P, T]) for p in range(2)]
        s0_sb = sb("s0_sb", [P, 2, T])
        min0 = sb("min0", [P, MT])
        sum0 = sb("sum0", [P, MT])
        r0 = sb("r0", [P, MT])
        p0 = sb("p0", [P, 5, T])
        p0_hi = sb("p0_hi", [P, 5, T], F32R)
        p0_lo = sb("p0_lo", [P, 5, T], F32R)
        wsum = [sb(f"wsum{p}", [P, T]) for p in range(2)]
        rowsum0 = sb("rowsum0", [P, TB])
        at0_hi, at0_lo = (sb(f"at0_{part}", [P, T], F32R) for part in ("hi", "lo"))
        xr = sb("xr", [P, TB, E])
        stats = sb("stats", [P, TB, 6])
        mv = sb("mv", [P, TB, 2])
        var_eps = sb("var_eps", [P, TB, 1])
        rstd = sb("rstd", [P, TB, 1])
        neg_half = sb("neg_half", [P, 2, 1])
        xhat = sb("xhat", [P, TB, E])
        y_res = sb("y_res", [P, TB, E])
        xhT = sb("xhT", [P, EC, T])
        qw1_hi = sb("qw1_hi", [P, T], F32R)
        qw1_lo = sb("qw1_lo", [P, T], F32R)
        c1 = sb("c1", [P, TB])
        max1 = sb("max1", [P, TB, len(chunks)])
        neg_max1 = sb("neg_max1", [P, TB])
        bias1 = sb("bias1", [P, TB])
        sum1 = sb("sum1", [P, 2, TB])
        sum1_all = sb("sum1_all", [P, TB])
        r1 = sb("r1", [P, TB])
        p1T_hi = sb("p1T_hi", [P, RING, T], F32R)
        p1T_lo = sb("p1T_lo", [P, RING, T], F32R)
        at1 = sb("at1", [P, T])

        ps_l0 = stack.enter_context(nc.psum_tensor("ps_l0", [P, 4 * BANK], F32))
        ps_s1 = stack.enter_context(nc.psum_tensor("ps_s1", [P, 4 * BANK], F32))
        ps_s0 = ps_l0[:, 0:2 * BANK].rearrange("p (k t) -> p k t", t=BANK)
        ps_acc0 = ps_l0[:, 2 * BANK:3 * BANK]
        ps_misc = ps_l0[:, 3 * BANK:4 * BANK]

        def s1_bank(k):
            return ps_s1[:, k * BANK:(k + 1) * BANK]

        def s1_banks(b, t):
            return (ps_l0 if last(b) and t % 2 else ps_s1)[:].rearrange("p (k m) -> p k m", m=BANK)

        ps_turn = [s1_bank(k) for k in range(3)]
        ps_y = [s1_bank(0), s1_bank(3)]
        ps_q1 = s1_bank(0)
        ps_out = [s1_bank(1), s1_bank(2)]
        ps_acc1 = s1_bank(3)

        ident_zero, ident_done, ones_done = sem("ident_zero"), sem("ident_done"), sem("ones_done")
        row1_made = sem("row1_made")
        w_loaded = [sem(f"w_loaded{n}") for n in range(2)]
        cols_loaded = [sem(f"cols_loaded{n}") for n in range(2)]
        wv_loaded = sem("wv_loaded")
        rows_loaded = sem("rows_loaded")
        cols_turned, cols_done = sem("cols_turned"), sem("cols_done")
        wT_turned, wT_copied, reps_done = sem("wT_turned"), sem("wT_copied"), sem("reps_done")
        made_ps, made_sb = sem("made_ps"), sem("made_sb")
        small_ps, small_sb = sem("small_ps"), sem("small_sb")
        x_loaded = [sem(f"x_loaded{p}") for p in range(2)]
        ctx_loaded = [sem(f"ctx_loaded{g}") for g in range(GROUPS)]
        out_free = [sem(f"out_free{h}") for h in range(2)]
        ctxT_ps, xT_ps, qw0_ps, cb_ps = sem("ctxT_ps"), sem("xT_ps"), sem("qw0_ps"), sem("cb_ps")
        s0_ps, pv0_ps, pred_ps = sem("s0_ps"), sem("pv0_ps"), sem("pred_ps")
        rowsum_ps = sem("rowsum_ps")
        xhT_ps, qw1_ps, s1_ps, p1T_ps, pv1_ps, out_ps = (
            sem("xhT_ps"), sem("qw1_ps"), sem("s1_ps"), sem("p1T_ps"), sem("pv1_ps"), sem("out_ps"))
        ctxT_hi_done, xT_done, qw0_hi_done, cb_done = (
            sem("ctxT_hi_done"), sem("xT_done"), sem("qw0_hi_done"), sem("cb_done"))
        exp0_done, at0_done = sem("exp0_done"), sem("at0_done")
        xhT_done, qw1_hi_done, exp1_done, at1_done = (
            sem("xhT_done"), sem("qw1_hi_done"), sem("exp1_done"), sem("at1_done"))
        ctx_hi_done, p0_hi_done, p1T_hi_done = sem("ctx_hi_done"), sem("p0_hi_done"), sem("p1T_hi_done")
        ctxT_lo_done, qw0_lo_done, s0_read, r0_done = (
            sem("ctxT_lo_done"), sem("qw0_lo_done"), sem("s0_read"), sem("r0_done"))
        sum1_done = sem("sum1_done")
        xT_lo_done, at0_lo_done = sem("xT_lo_done"), sem("at0_lo_done")
        weights_lo_done, wv0_hi_done = sem("weights_lo_done"), sem("wv0_hi_done")
        rowsum_done, xbias_done = sem("rowsum_done"), sem("xbias_done")
        p0_lo_done, p1T_lo_done = sem("p0_lo_done"), sem("p1T_lo_done")
        xr_done, stats_done, mv_done, rstd_done, xhat_done = (
            sem("xr_done"), sem("stats_done"), sem("mv_done"), sem("rstd_done"), sem("xhat_done"))
        c1_done, qw1_lo_done, max1_done, neg_max1_done, bias1_done, r1_done, o_done = (
            sem("c1_done"), sem("qw1_lo_done"), sem("max1_done"), sem("neg_max1_done"), sem("bias1_done"),
            sem("r1_done"), sem("o_done"))
        var_done, wsum_part = sem("var_done"), sem("wsum_part")
        ctx_lo_done, wsum_done, y_part_done, y_res_done = (
            sem("ctx_lo_done"), sem("wsum_done"), sem("y_part_done"), sem("y_res_done"))

        apart_regs = {eng: eng.alloc_register("apart") for eng in (nc.vector, nc.gpsimd)}

        def wait_apart(eng, semaphore, value):
            if not isinstance(value, int):
                apart_reg = apart_regs[eng]
                eng.reg_mov(apart_reg, value)
                value = eng.snap(apart_reg, min_val=1)
            eng.wait_ge(ident_done, 1)
            eng.wait_ge(semaphore, value)

        blk = stack.enter_context(nc.Block())

        AHEAD = {("turn_x", 0), ("x_turned", 0), ("turn_x", 1), ("x_turned", 1), ("xT_low", 0), ("xT_low", 1),
                 ("turn_ctx", 0), ("ctx_high", 0), ("ctxT_low", 0)}

        def run(body, pre, eng):
            pre[0]()
            body(None, None, batch(0, 0), AHEAD)
            pre[1]()
            body(batch(0, 0), None, batch(0, 1))
            with eng.Fori(0, PAIRS) as pair:
                body(batch(pair, 1), batch(pair, 0), batch(pair, 2))
                body(batch(pair, 2), batch(pair, 1), batch(pair, 3))
            body(batch(PAIRS, 1), batch(PAIRS, 0), None)
            body(None, batch(PAIRS, 1), None)

        @blk.sync
        def _(sp):
            def load_x(c):
                sp.dma_start(x_sb[c.par][:], x[bass.ds(c.n, 1)].rearrange("o (t p) e -> p (o t) e", p=P)
                             ).then_inc(x_loaded[c.par], 16)

            def load_ctx(c, g, after=None):
                if after is not None:
                    sp.wait_ge(ctxT_ps, GROUPS * (c.n - 1) + g + 1)
                    sp.wait_ge(ctx_lo_done, GROUPS * (c.n - 1) + g + 1)
                full = [i for i in group(g) if rows(i) == P]
                dst = ctx_sb
                if full:
                    src = ctx[bass.ds(c.n, 1), full[0] * P:(full[-1] + 1) * P, :]
                    sp.dma_start(dst[:, full[0]:full[-1] + 1, :], src.rearrange("o (i p) l -> p (o i) l", p=P)
                                 ).then_inc(ctx_loaded[g], 16)
                else:
                    i = group(g)[0]
                    src = ctx[bass.ds(c.n, 1), i * P:M, :]
                    sp.dma_start(dst[0:rows(i), i, :], src.rearrange("o p l -> (o p) l")
                                 ).then_inc(ctx_loaded[g], 16)

            def pre0():
                sp.dma_start(wq_sb[0], wq0.rearrange("(c p) h -> p c h", p=P)).then_inc(w_loaded[0], 16)
                sp.dma_start(wk_sb[0], wk0).then_inc(w_loaded[0], 16)
                load_x(batch(0, 0))
                for g in range(GROUPS):
                    load_ctx(batch(0, 0), g)
                sp.dma_start(wq_sb[1], wq1.rearrange("(c p) h -> p c h", p=P)).then_inc(w_loaded[1], 16)
                sp.dma_start(wk_sb[1], wk1).then_inc(w_loaded[1], 16)
                for k, v in enumerate((bq1, bk1, bv1, gamma, beta)):
                    sp.dma_start(vec_rows[1][k:k + 1, :], v.rearrange("(o e) -> o e", o=1)).then_inc(cols_loaded[1], 16)
                load_x(batch(0, 1))
                sp.dma_start(wv0_sb, wv0).then_inc(wv_loaded, 16)
                sp.dma_start(wv1_sb, wv1).then_inc(wv_loaded, 16)
                sp.dma_start(wo_sb, wo.rearrange("(c p) d -> p c d", p=P)).then_inc(wv_loaded, 16)
                for row, v, landed in ((bv0_row[:], bv0, rows_loaded), (gamma_row[:], gamma, rows_loaded),
                                       (beta_row, beta, out_free[0]), (bo_row, bo, out_free[1])):
                    sp.dma_start(row, v.rearrange("(o e) -> o e", o=1).broadcast_to([P, E])).then_inc(landed, 16)

            def pre1():
                pass

            def body(a, b, c, done=()):
                if a and c:
                    for g in range(GROUPS):
                        load_ctx(c, g, after=True)
                if b is None:
                    return
                dst = out[bass.ds(b.n, 1)].rearrange("o (t p) e -> p (o t) e", p=P)
                for h in range(2):
                    sp.wait_ge(o_done, 2 * b.n + h + 1)
                    sp.dma_start(dst[:, 2 * h:2 * h + 2, :], y_res[:, 2 * h:2 * h + 2, :]
                                 ).then_inc(out_free[h], 16)

            run(body, (pre0, pre1), sp)
            for h in range(2):
                sp.wait_ge(out_free[h], 16 * (B + 1))

        @blk.tensor
        def _(pe):
            def split3(ps, w_hi, w_lo, m_hi, m_lo, start=True, stop=True):
                nc.tensor.matmul(ps, w_lo, m_hi, start=start, stop=False)
                nc.tensor.matmul(ps, w_hi, m_lo, start=False, stop=False)
                return nc.tensor.matmul(ps, w_hi, m_hi, start=False, stop=stop)

            def turn_ctx(a, g):
                pe.wait_ge(ctx_loaded[g], 16 * (a.n + 1))
                for k, i in enumerate(group(g)):
                    m = rows(i)
                    mm = nc.tensor.transpose(ps_misc[:, k * P:k * P + m], ctx_sb[0:m, i, :],
                                             ident[0:m, 0:m])
                mm.then_inc(ctxT_ps, 1)

            def turn_x(a, c, ps=ps_misc):
                if c == 0:
                    pe.wait_ge(x_loaded[a.par], 16 * (a.use + 1))
                for t in range(TB):
                    mm = nc.tensor.transpose(ps[:, t * P:(t + 1) * P], x_sb[a.par][:, t, c * P:(c + 1) * P],
                                             ident[:])
                mm.then_inc(xT_ps, 1)

            def project_q0(a, _):
                pe.wait_ge(xT_lo_done, EC * (a.n + 1))
                for c in range(EC):
                    mm = split3(ps_misc[:], a0_hi[:, c, :], a0_lo[:, c, :], xT_hi[:, c, :], xT_lo[:, c, :],
                                start=(c == 0), stop=(c == EC - 1))
                mm.then_inc(qw0_ps, 1)

            def project_bias0(a, _):
                for c in range(EC):
                    mm = split3(ps_misc[:], u0_hi[:, c, :], u0_lo[:, c, :], xT_hi[:, c, :], xT_lo[:, c, :],
                                start=(c == 0), stop=(c == EC - 1))
                mm.then_inc(cb_ps, 1)

            def scores0(a, i):
                if i % TB == 0:
                    pe.wait_ge(ctxT_lo_done, GROUPS * a.n + i // TB + 1)
                if i == 0:
                    pe.wait_ge(qw0_lo_done, a.n + 1)
                if i >= 2 or not first(a):
                    pe.wait_ge(s0_read, MT * a.n + i - 1)
                m = slice(i * P, i * P + rows(i))
                split3(ps_s0[0:rows(i), (a.par + i) % 2, :], ctxT_hi[a.par][:, m], ctxT_lo[a.par][:, m],
                       qw0_hi[a.par][:], qw0_lo[a.par][:]).then_inc(s0_ps, 1)

            def weigh0(a, i):
                pe.wait_ge(p0_lo_done, MT * a.n + i + 1)
                if i % TB == 0:
                    pe.wait_ge(ctx_lo_done, GROUPS * a.n + i // TB + 1)
                if i == 0 and not first(a):
                    pe.wait_ge(at0_lo_done, a.n)
                m = rows(i)
                split3(ps_acc0[:], ctx_hi[a.par][0:m, i, :], ctx_lo[a.par][0:m, i, :], p0_hi[0:m, ring0(i), :],
                       p0_lo[0:m, ring0(i), :], start=(i == 0), stop=(i == MT - 1)).then_inc(pv0_ps, 1)

            def sum_rows0(a, _):
                pe.wait_ge(wsum_done, MT * (a.n + 1))
                for t in range(TB):
                    mm = nc.tensor.matmul(ps_misc[:, t:t + 1], wsum[a.par][:, t * P:(t + 1) * P], ones[:, 0:1],
                                          start=True, stop=True)
                mm.then_inc(rowsum_ps, 1)

            def predict(a, h):
                if h == 0:
                    pe.wait_ge(at0_lo_done, a.n + 1)
                for k in range(2):
                    t = slice((2 * h + k) * P, (2 * h + k + 1) * P)
                    mm = split3(ps_misc[:, k * E:(k + 1) * E], at0_hi[:, t], at0_lo[:, t], wv0_hi[:], wv0_lo[:])
                mm.then_inc(pred_ps, 1)

            def turn_y(b, c):
                pe.wait_ge(xhat_done, TB * (b.n + 1))
                if c == 0:
                    pe.wait_ge(row1_made, MADE)
                    pe.wait_ge(weights_lo_done, 3)
                for t in range(TB):
                    mm = nc.tensor.transpose(ps_y[c][:, t * P:(t + 1) * P], xhat[:, t, c * P:(c + 1) * P], ident[:])
                mm.then_inc(xhT_ps, 1)

            def project_q1(b, _):
                pe.wait_ge(xhT_done, EC * (b.n + 1))
                for c in range(EC):
                    mm = nc.tensor.matmul(ps_q1, a1_gamma[:, c, :], xhT[:, c, :], start=(c == 0), stop=(c == EC - 1))
                mm.then_inc(qw1_ps, 1)

            def scores1(b, i):
                t, k = i // len(chunks), i % len(chunks)
                if i == 0:
                    pe.wait_ge(qw1_lo_done, b.n + 1)
                before = t - 2 if last(b) else t - 1
                if before >= 0 and k in (0, len(chunks) - 1):
                    pe.wait_ge(exp1_done, 2 * (TB * b.n + before) + (1 if k == 0 else 2))
                q = slice(t * P, (t + 1) * P)
                lo, hi = chunks[k]
                split3(s1_banks(b, t)[:, k, 0:hi - lo], qw1_hi[:, q], qw1_lo[:, q], ctxT_hi[b.par][:, lo:hi],
                       ctxT_lo[b.par][:, lo:hi]).then_inc(s1_ps, 1)

            def turn_p1(b, i):
                if i == 0:
                    pe.wait_ge(exp1_done, 2 * TB * (b.n + 1))
                elif i >= 3:
                    pe.wait_ge(p1T_lo_done, MT * b.n + i - 2)
                m = rows(i)
                for t in range(TB):
                    mm = nc.tensor.transpose(ps_turn[i % 3][0:m, t * P:(t + 1) * P], p1[:, t, i * P:i * P + m], ident[:])
                mm.then_inc(p1T_ps, 1)

            def weigh1(b, i):
                pe.wait_ge(p1T_lo_done, MT * b.n + i + 1)
                m = rows(i)
                split3(ps_acc1, ctx_hi[b.par][0:m, i, :], ctx_lo[b.par][0:m, i, :], p1T_hi[0:m, i % RING, :],
                       p1T_lo[0:m, i % RING, :], start=(i == 0), stop=(i == MT - 1)).then_inc(pv1_ps, 1)

            def project_out(b, h):
                if h == 0:
                    pe.wait_ge(at1_done, b.n + 1)
                for k in range(2):
                    t = slice((2 * h + k) * P, (2 * h + k + 1) * P)
                    mm = nc.tensor.matmul(ps_out[h][:, k * E:(k + 1) * E], at1[:, t], w2_sb[:], start=True, stop=True)
                mm.then_inc(out_ps, 1)

            def turn_weights(n, ps_q, ps_k):
                pe.wait_ge(w_loaded[n], 16 * 2)
                for h in range(EC):
                    for c in range(EC):
                        mm = nc.tensor.transpose(ps_q[:, h * E + c * P:h * E + (c + 1) * P],
                                                 wq_sb[n][:, c, h * P:(h + 1) * P], ident[:])
                mm.then_inc(wT_turned, 1)
                for h in range(EC):
                    mm = nc.tensor.transpose(ps_k[:, h * P:(h + 1) * P], wk_sb[n][:, h * P:(h + 1) * P], ident[:])
                mm.then_inc(wT_turned, 1)

            def turn_vectors(n, ps):
                pe.wait_ge(cols_loaded[n], 16 * NV[n])
                for c in range(EC):
                    mm = nc.tensor.transpose(ps[:, c * NV[n]:(c + 1) * NV[n]], vec_rows[n][:, c * P:(c + 1) * P],
                                             ident[0:NV[n], 0:NV[n]])
                mm.then_inc(cols_turned, 1)

            def make_a(n, ps):
                for c in range(EC):
                    for h in range(EC):
                        mm = nc.tensor.matmul(ps[:, c * P:(c + 1) * P], wqT[n][:, h, c * P:(c + 1) * P],
                                              wkT[:, n, h, :], start=(h == 0), stop=(h == EC - 1))
                return mm

            def keep_warm(n):
                for _ in range(n):
                    nc.tensor.matmul(ps_s0[:, 0, 0:P], ident[:], ident[:], start=True, stop=True)

            def pre0():
                pe.wait_ge(ident_done, 1)
                keep_warm(WARM[0])
                turn_weights(0, s1_bank(0), s1_bank(1))
                turn_vectors(0, ps_acc0)
                turn_x(batch(0, 0), 0)
                turn_x(batch(0, 0), 1, s1_bank(3))
                keep_warm(WARM[1])
                pe.wait_ge(wT_copied, 2)
                make_a(0, s1_bank(2))
                pe.wait_ge(reps_done, EC)
                for c in range(EC):
                    for h in range(EC):
                        mm = nc.tensor.matmul(s1_bank(2)[:, E + c * P:E + (c + 1) * P], wqT[0][:, h, c * P:(c + 1) * P],
                                              bk_rep[0][:, h, :], start=(h == 0), stop=(h == EC - 1))
                mm.then_inc(made_ps, 1)
                for h in range(EC):
                    nc.tensor.matmul(ps_acc0[:, 0:1], wkT[:, 0, h, :], bq_col[0][:, h:h + 1],
                                     start=(h == 0), stop=(h == EC - 1))
                for h in range(EC):
                    mm = nc.tensor.matmul(ps_acc0[:, 1:2], bk_rep[0][:, h, :], bq_col[0][:, h:h + 1],
                                          start=(h == 0), stop=(h == EC - 1))
                mm.then_inc(small_ps, 1)
                pe.wait_ge(xT_lo_done, 1)
                turn_ctx(batch(0, 0), 0)
                keep_warm(WARM[2])
                pe.wait_ge(small_sb, 1)
                pe.wait_ge(weights_lo_done, 2)
                pe.wait_ge(xT_lo_done, EC)
                pe.wait_ge(ctxT_lo_done, 1)

            def pre1():
                turn_weights(1, s1_bank(0), s1_bank(1))
                pe.wait_ge(wv_loaded, 16 * 3)
                for h in range(EC):
                    mm = nc.tensor.transpose(s1_bank(1)[:, E + h * P:E + (h + 1) * P], wv1_sb[:, h * P:(h + 1) * P], ident[:])
                mm.then_inc(wT_turned, 1)
                turn_vectors(1, s1_bank(3))
                pe.wait_ge(wT_copied, 5)
                make_a(1, s1_bank(2))
                pe.wait_ge(reps_done, 3 * EC)
                for h in range(EC):
                    mm = nc.tensor.matmul(s1_bank(2)[:, E:2 * E], bk_rep[1][:, h, :], wqT[1][:, h, :],
                                          start=(h == 0), stop=(h == EC - 1))
                mm.then_inc(made_ps, 1)
                for h in range(EC):
                    nc.tensor.matmul(s1_bank(3)[:, 0:E], wvT[:, h, :], wo_sb[:, h, :], start=(h == 0), stop=(h == EC - 1))
                for h in range(EC):
                    mm = nc.tensor.matmul(s1_bank(3)[:, E:2 * E], bv1_rep[:, h, :], wo_sb[:, h, :],
                                          start=(h == 0), stop=(h == EC - 1))
                mm.then_inc(made_ps, 1)
                for h in range(EC):
                    nc.tensor.matmul(s1_bank(0)[:, 1:2], bk_rep[1][:, h, :], bq_col[1][:, h:h + 1],
                                     start=(h == 0), stop=(h == EC - 1))
                for h in range(EC):
                    nc.tensor.matmul(s1_bank(0)[:, 0:1], wkT[:, 1, h, :], bq_col[1][:, h:h + 1], start=(h == 0), stop=False)
                pe.wait_ge(made_sb, 3)
                for c in range(EC):
                    mm = nc.tensor.matmul(s1_bank(0)[:, 0:1], a1_sb[:, c, :], beta_col[:, c:c + 1], start=False,
                                          stop=(c == EC - 1))
                mm.then_inc(small_ps, 1)

            MISC = ("turn_x", "project_q0", "project_bias0", "turn_ctx", "sum_rows0", "predict")

            def misc_read(step, a, b, c, done):
                here = [(n, {"a": a, "b": b, "c": c}[who], i) for n, who, i in TENSOR_ORDER[:step]
                        if n in MISC and (n, i) not in done]
                before = [(n, {"a": b, "c": a}[who], i) for n, who, i in TENSOR_ORDER if n in MISC]
                for n, bt, i in reversed(before + here):
                    if bt:
                        break
                else:
                    return
                if n == "turn_x":
                    pe.wait_ge(xT_lo_done, EC * bt.n + i + 1)
                elif n == "project_q0":
                    pe.wait_ge(qw0_lo_done, bt.n + 1)
                elif n == "project_bias0":
                    pe.wait_ge(cb_done, bt.n + 1)
                elif n == "sum_rows0":
                    pe.wait_ge(rowsum_done, bt.n + 1)
                elif n == "turn_ctx":
                    pe.wait_ge(ctxT_lo_done, GROUPS * bt.n + i + 1)
                else:
                    pe.wait_ge(xr_done, 2 * bt.n + i + 1)

            steps = {f.__name__: f for f in (
                turn_x, project_q0, project_bias0, turn_ctx, scores0, weigh0, sum_rows0, predict, turn_y, project_q1, scores1, turn_p1, weigh1, project_out)}

            def body(a, b, c, done=()):
                for step, (name, who, i) in enumerate(TENSOR_ORDER):
                    bt = {"a": a, "b": b, "c": c}[who]
                    if bt and (name, i) not in done:
                        if name in MISC:
                            misc_read(step, a, b, c, done)
                        steps[name](bt, i)

            run(body, (pre0, pre1), pe)

        @blk.scalar
        def _(act):
            def ctx_high(a, g):
                act.wait_ge(ctxT_ps, GROUPS * a.n + g + 1)
                lo, hi = group_cols(g)
                nc.scalar.copy(ctxT_hi[a.par][:, lo:hi], ps_misc[:, 0:hi - lo]).then_inc(ctxT_hi_done, 1)

            def ctx_split(a, g):
                act.wait_ge(ctx_loaded[g], 16 * (a.n + 1))
                if g == 0 and not (isinstance(a.n, int) and a.n < 2):
                    act.wait_ge(pv1_ps, MT * (a.n - 2) + group(g)[-1] + 1)
                m = rows(group(g)[0])
                tiles = slice(group(g)[0], group(g)[-1] + 1)
                nc.scalar.copy(ctx_hi[a.par][0:m, tiles, :], ctx_sb[0:m, tiles, :]).then_inc(ctx_hi_done, 1)

            def load_x(a, _):
                if isinstance(a.n, int) and a.n < 2:
                    return
                act.wait_ge(xbias_done, a.n - 1)
                act.dma_start(x_sb[a.par][:], x[bass.ds(a.n, 1)].rearrange("o (t p) e -> p (o t) e", p=P)
                              ).then_inc(x_loaded[a.par], 16)

            def x_turned(a, c, ps=ps_misc):
                act.wait_ge(xT_ps, EC * a.n + c + 1)
                if c == 0 and not first(a):
                    act.wait_ge(cb_ps, a.n)
                nc.scalar.copy(xT_hi[:, c, :], ps[:]).then_inc(xT_done, 1)

            def q0_high(a, _):
                act.wait_ge(qw0_ps, a.n + 1)
                nc.scalar.activation(qw0_hi[a.par][:], ps_misc[:], ACT.Identity, bias=qb0, scale=1.0
                                     ).then_inc(qw0_hi_done, 1)

            def bias0(a, _):
                act.wait_ge(cb_ps, a.n + 1)
                nc.scalar.activation(cb[a.par][:], ps_misc[:], ACT.Identity, bias=bqbk0, scale=1.0
                                     ).then_inc(cb_done, 1)

            def exp0(a, i):
                act.wait_ge(s0_read, MT * a.n + i + 1)
                if (n := before0(a, i)) is not None:
                    act.wait_ge(p0_lo_done, n)
                m = rows(i)
                nc.scalar.activation(p0[0:m, ring0(i), :], s0_sb[0:m, (a.par + i) % 2, :], ACT.Exp, bias=min0[0:m, i:i + 1],
                                     scale=-1.0, accum_out=sum0[0:m, i:i + 1]).then_inc(exp0_done, 1)

            def p0_high(a, i):
                act.wait_ge(r0_done, MT * a.n + i + 1)
                if (n := before0(a, i)) is not None:
                    act.wait_ge(pv0_ps, n)
                    act.wait_ge(wsum_done, n)
                m = rows(i)
                nc.scalar.activation(p0_hi[0:m, ring0(i), :], p0[0:m, ring0(i), :], ACT.Copy, scale=r0[0:m, i:i + 1]
                                     ).then_inc(p0_hi_done, 1)

            def weighed0(a, _):
                act.wait_ge(pv0_ps, MT * (a.n + 1))
                if not first(a):
                    act.wait_ge(pred_ps, 2 * a.n)
                nc.scalar.copy(at0_hi[:], ps_acc0[:]).then_inc(at0_done, 1)

            def y_turned(b, c):
                act.wait_ge(xhT_ps, EC * b.n + c + 1)
                if c == 0:
                    act.wait_ge(row1_made, MADE)
                nc.scalar.copy(xhT[:, c, :], ps_y[c]).then_inc(xhT_done, 1)

            def q1_high(b, _):
                act.wait_ge(qw1_ps, b.n + 1)
                nc.scalar.activation(qw1_hi[:], ps_q1, ACT.Identity, bias=scaled1[:, 0:1], scale=1.0
                                     ).then_inc(qw1_hi_done, 1)

            def exp1(b, i):
                t, h = i // 2, i % 2
                if h == 0:
                    act.wait_ge(bias1_done, TB * b.n + t + 1)
                if h == 0:
                    scores = s1_banks(b, t)[:, 0:len(chunks) - 1, 0:CHUNK]
                    exps = p1[:, t, 0:last_lo].rearrange("p (k m) -> p k m", m=CHUNK)
                else:
                    scores, exps = s1_banks(b, t)[:, len(chunks) - 1, 0:M - last_lo], p1[:, t, last_lo:M]
                nc.scalar.activation(exps, scores, ACT.Exp, bias=bias1[:, t:t + 1], scale=1.0,
                                     accum_out=sum1[:, h, t:t + 1]).then_inc(exp1_done, 1)

            def p1_turned(b, i):
                act.wait_ge(p1T_ps, MT * b.n + i + 1)
                if i >= RING:
                    act.wait_ge(pv1_ps, MT * b.n + i + 1 - RING)
                m = rows(i)
                nc.scalar.copy(p1T_hi[0:m, i % RING, :], ps_turn[i % 3][0:m, :]).then_inc(p1T_hi_done, 1)

            def weighed1(b, _):
                act.wait_ge(pv1_ps, MT * (b.n + 1))
                nc.scalar.copy(at1[:], ps_acc1).then_inc(at1_done, 1)

            def pre0():
                for k, v in enumerate((bq0, bk0)):
                    act.dma_start(vec_rows[0][k:k + 1, :], v.rearrange("(o e) -> o e", o=1)).then_inc(cols_loaded[0], 16)
                act.wait_ge(wT_turned, 1)
                nc.scalar.copy(wqT[0].rearrange("p h e -> p (h e)"), s1_bank(0)).then_inc(wT_copied, 1)
                act.wait_ge(wT_turned, 2)
                nc.scalar.copy(wkT[:, 0].rearrange("p h l -> p (h l)"), s1_bank(1)[:, 0:E]).then_inc(wT_copied, 1)
                x_turned(batch(0, 0), 0)
                x_turned(batch(0, 0), 1, s1_bank(3))
                act.wait_ge(made_ps, 1)
                nc.scalar.copy(a0_hi[:].rearrange("p c l -> p (c l)"), s1_bank(2)[:, 0:E]).then_inc(made_sb, 1)
                nc.scalar.copy(u0_hi[:].rearrange("p c l -> p (c l)"), s1_bank(2)[:, E:2 * E]).then_inc(made_sb, 1)
                act.wait_ge(small_ps, 1)
                nc.scalar.copy(small[0][:], ps_acc0[:, 0:2]).then_inc(small_sb, 1)
                ctx_high(batch(0, 0), 0)
                act.wait_ge(small_sb, 1)

            def pre1():
                act.wait_ge(wv_loaded, 16 * 3)
                nc.scalar.copy(wv0_hi[:], wv0_sb).then_inc(wv0_hi_done, 1)
                act.wait_ge(wT_turned, 3)
                nc.scalar.copy(wqT[1].rearrange("p h e -> p (h e)"), s1_bank(0)).then_inc(wT_copied, 1)
                act.wait_ge(wT_turned, 5)
                nc.scalar.copy(wkT[:, 1].rearrange("p h l -> p (h l)"), s1_bank(1)[:, 0:E]).then_inc(wT_copied, 1)
                nc.scalar.copy(wvT.rearrange("p h l -> p (h l)"), s1_bank(1)[:, E:2 * E]).then_inc(wT_copied, 1)
                act.wait_ge(made_ps, 2)
                nc.scalar.copy(a1_sb[:].rearrange("p c l -> p (c l)"), s1_bank(2)[:, 0:E]).then_inc(made_sb, 1)
                nc.scalar.copy(u1_row, s1_bank(2)[:, E:2 * E]).then_inc(made_sb, 1)
                act.wait_ge(made_ps, 3)
                nc.scalar.copy(w2_sb[:], s1_bank(3)[:, 0:E]).then_inc(made_sb, 1)
                act.wait_ge(small_ps, 2)
                nc.scalar.copy(small[1][:], s1_bank(0)[:, 0:2]).then_inc(small_sb, 1)

            steps = {f.__name__: f for f in (
                load_x, x_turned, q0_high, bias0, ctx_high, ctx_split, exp0, p0_high, weighed0, y_turned, q1_high, exp1, p1_turned, weighed1)}

            def body(a, b, c, done=()):
                for name, who, i in SCALAR_ORDER:
                    bt = {"a": a, "b": b, "c": c}[who]
                    if bt and (name, i) not in done:
                        steps[name](bt, i)

            run(body, (pre0, pre1), act)

        @blk.vector
        def _(dve):
            def ctxT_low(a, g):
                dve.wait_ge(ctxT_hi_done, GROUPS * a.n + g + 1)
                lo, hi = group_cols(g)
                nc.vector.tensor_tensor(ctxT_lo[a.par][:, lo:hi], ps_misc[:, 0:hi - lo],
                                        ctxT_hi[a.par][:, lo:hi].bitcast(F32), ALU.subtract).then_inc(ctxT_lo_done, 1)

            def xT_low(a, c, ps=ps_misc):
                dve.wait_ge(xT_done, EC * a.n + c + 1)
                nc.vector.tensor_tensor(xT_lo[:, c, :], ps[:], xT_hi[:, c, :].bitcast(F32), ALU.subtract
                                        ).then_inc(xT_lo_done, 1)

            def at0_low(a, _):
                dve.wait_ge(at0_done, a.n + 1)
                nc.vector.tensor_tensor(at0_lo[:], ps_acc0[:], at0_hi[:].bitcast(F32), ALU.subtract
                                        ).then_inc(at0_lo_done, 1)

            def weight_low(lo, exact, hi):
                nc.vector.tensor_tensor(lo, exact, hi.bitcast(F32), ALU.subtract).then_inc(weights_lo_done, 1)

            def q0_low(a, _):
                dve.wait_ge(qw0_hi_done, a.n + 1)
                nc.vector.scalar_tensor_tensor(qw0_lo[a.par][:], ps_misc[:], qb0, qw0_hi[a.par][:].bitcast(F32),
                                               ALU.add, ALU.subtract).then_inc(qw0_lo_done, 1)

            def max0(a, i):
                if i == 0:
                    dve.wait_ge(cb_done, a.n + 1)
                if i >= 2 or not first(a):
                    dve.wait_ge(exp0_done, MT * a.n + i - 1)
                wait_apart(dve, s0_ps, MT * a.n + i + 1)
                m = rows(i)
                nc.vector.tensor_tensor_reduce(out=s0_sb[0:m, (a.par + i) % 2, :], in0=ps_s0[0:m, (a.par + i) % 2, :], in1=cb[a.par][0:m, :],
                                               scale=-SCALE, scalar=BIG, op0=ALU.add, op1=ALU.min,
                                               accum_out=min0[0:m, i:i + 1]).then_inc(s0_read, 1)

            def recip0(a, i):
                dve.wait_ge(exp0_done, MT * a.n + i + 1)
                m = rows(i)
                nc.vector.reciprocal(r0[0:m, i:i + 1], sum0[0:m, i:i + 1]).then_inc(r0_done, 1)

            def p0_low(a, i):
                dve.wait_ge(p0_hi_done, MT * a.n + i + 1)
                m = rows(i)
                nc.vector.scalar_tensor_tensor(p0_lo[0:m, ring0(i), :], p0[0:m, ring0(i), :], r0[0:m, i:i + 1],
                                               p0_hi[0:m, ring0(i), :].bitcast(F32), ALU.mult, ALU.subtract
                                               ).then_inc(p0_lo_done, 1)

            def p1_low(b, i):
                dve.wait_ge(p1T_hi_done, MT * b.n + i + 1)
                m = rows(i)
                nc.vector.tensor_tensor(p1T_lo[0:m, i % RING, :], ps_turn[i % 3][0:m, :],
                                        p1T_hi[0:m, i % RING, :].bitcast(F32), ALU.subtract).then_inc(p1T_lo_done, 1)

            def bias_x0(a, _):
                dve.wait_ge(rowsum_ps, a.n + 1)
                nc.vector.tensor_copy(rowsum0[:], ps_misc[:, 0:TB]).then_inc(rowsum_done, 1)
                if first(a):
                    dve.wait_ge(rows_loaded, 16 * 2)
                    dve.wait_ge(row1_made, MADE)
                else:
                    dve.wait_ge(c1_done, TB * a.n)
                dve.wait_ge(x_loaded[a.par], 16 * (a.use + 1))
                dve.wait_ge(rowsum_done, a.n + 1)
                for t in range(TB):
                    ins = nc.vector.scalar_tensor_tensor(xr[:, t, :], bv0_row[:], rowsum0[:, t:t + 1], x_sb[a.par][:, t, :],
                                                         ALU.mult, ALU.add)
                ins.then_inc(xbias_done, 1)

            def residual0(a, h):
                two = slice(2 * h, 2 * h + 2)
                if h == 0:
                    dve.wait_ge(xbias_done, a.n + 1)
                dve.wait_ge(pred_ps, 2 * a.n + h + 1)
                nc.vector.tensor_tensor(xr[:, two, :], ps_misc[:].rearrange("p (t e) -> p t e", e=E),
                                        xr[:, two, :], ALU.add).then_inc(xr_done, 1)

            def moments0(a, h):
                two = slice(2 * h, 2 * h + 2)
                dve.wait_ge(xr_done, 2 * a.n + h + 1)
                for t in (2 * h, 2 * h + 1):
                    nc.vector.bn_stats(stats[:, t, :], xr[:, t, :]).then_inc(stats_done, 1)
                for t in (2 * h, 2 * h + 1):
                    wait_apart(dve, stats_done, TB * a.n + t + 1)
                    nc.vector.bn_aggr(mv[:, t, :], stats[:, t, :]).then_inc(mv_done, 1)
                dve.wait_ge(mv_done, TB * a.n + 2 * h + 2)
                nc.vector.tensor_scalar(var_eps[:, two, :], mv[:, two, 1:2], LN_EPS, None, ALU.add).then_inc(var_done, 1)

            def normalised(a, h):
                dve.wait_ge(rstd_done, 2 * a.n + h + 1)
                if h == 0 and not first(a):
                    dve.wait_ge(xhT_ps, EC * a.n)
                    dve.wait_ge(y_part_done, a.n)
                for t in (2 * h, 2 * h + 1):
                    nc.vector.tensor_scalar(xhat[:, t, :], xr[:, t, :], mv[:, t, 0:1], rstd[:, t, :], ALU.subtract,
                                            ALU.mult).then_inc(xhat_done, 1)

            def bias_row1(b, _):
                dve.wait_ge(row1_made, MADE)
                dve.wait_ge(xhat_done, TB * (b.n + 1))
                for t in range(TB):
                    nc.vector.tensor_tensor_reduce(out=xr[:, t, :], in0=xhat[:, t, :], in1=u1_gamma[:], scale=1.0,
                                                   scalar=c1_const[:, 0:1], op0=ALU.mult, op1=ALU.add,
                                                   accum_out=c1[:, t:t + 1]).then_inc(c1_done, 1)

            def q1_low(b, _):
                dve.wait_ge(qw1_hi_done, b.n + 1)
                nc.vector.scalar_tensor_tensor(qw1_lo[:], ps_q1, scaled1[:, 0:1], qw1_hi[:].bitcast(F32), ALU.add,
                                               ALU.subtract).then_inc(qw1_lo_done, 1)

            def rowmax1(b, i):
                t, k = i // len(chunks), i % len(chunks)
                lo, hi = chunks[k]
                dve.wait_ge(s1_ps, len(chunks) * TB * b.n + i + 1)
                nc.vector.tensor_reduce(max1[:, t, k:k + 1], s1_banks(b, t)[:, k, 0:min(hi, M) - lo], AX_X, ALU.max
                                        ).then_inc(max1_done, 1)

            def bias1_of(b, t):
                if t == 0:
                    dve.wait_ge(c1_done, TB * (b.n + 1))
                dve.wait_ge(max1_done, len(chunks) * (TB * b.n + t + 1))
                nc.vector.tensor_reduce(neg_max1[:, t:t + 1], max1[:, t, :], AX_X, ALU.max, negate=True
                                        ).then_inc(neg_max1_done, 1)
                dve.wait_ge(neg_max1_done, TB * b.n + t + 1)
                nc.vector.scalar_tensor_tensor(bias1[:, t:t + 1], neg_max1[:, t:t + 1], c1[:, t:t + 1], c1[:, t:t + 1],
                                               ALU.subtract, ALU.add).then_inc(bias1_done, 1)

            def recip1(b, _):
                dve.wait_ge(exp1_done, 2 * TB * (b.n + 1))
                nc.vector.tensor_tensor(sum1_all[:], sum1[:, 0, :], sum1[:, 1, :], ALU.add).then_inc(sum1_done, 1)
                dve.wait_ge(sum1_done, b.n + 1)
                nc.vector.reciprocal(r1[:], sum1_all[:]).then_inc(r1_done, 1)

            def finish(b, h):
                if h == 0:
                    dve.wait_ge(r1_done, b.n + 1)
                    dve.wait_ge(y_res_done, b.n + 1)
                dve.wait_ge(out_ps, 2 * b.n + h + 1)
                for k in range(2):
                    t = 2 * h + k
                    ins = nc.vector.scalar_tensor_tensor(y_res[:, t, :], ps_out[h][:, k * E:(k + 1) * E], r1[:, t:t + 1],
                                                         y_res[:, t, :], ALU.mult, ALU.add)
                ins.then_inc(o_done, 1)

            def repeat(n, ps, reps):
                dve.wait_ge(cols_turned, n + 1)
                nc.vector.tensor_copy(cols[n][:].rearrange("p c n -> p (c n)"), ps[:, 0:EC * NV[n]]).then_inc(cols_done, 1)
                dve.wait_ge(cols_done, n + 1)
                for rep, col in reps:
                    for h in range(EC):
                        nc.vector.tensor_scalar(rep[:, h, :], ones[:], col[:, h:h + 1], None, ALU.mult
                                                ).then_inc(reps_done, 1)

            def pre0():
                for p in range(2):
                    nc.vector.memset(ctxT_hi[p][:, M:MPAD].bitcast(F32), 0.0)
                    nc.vector.memset(ctxT_lo[p][:, M:MPAD].bitcast(F32), 0.0)
                nc.vector.memset(ones[:], 1.0).then_inc(ones_done, 1)
                dve.wait_ge(ones_done, 1)
                repeat(0, ps_acc0, ((bk_rep[0], bk_col[0]),))
                xT_low(batch(0, 0), 0)
                xT_low(batch(0, 0), 1, s1_bank(3))
                dve.wait_ge(made_sb, 2)
                weight_low(a0_lo[:].rearrange("p c l -> p (c l)"), s1_bank(2)[:, 0:E], a0_hi[:].rearrange("p c l -> p (c l)"))
                weight_low(u0_lo[:].rearrange("p c l -> p (c l)"), s1_bank(2)[:, E:2 * E],
                           u0_hi[:].rearrange("p c l -> p (c l)"))
                ctxT_low(batch(0, 0), 0)
                dve.wait_ge(small_sb, 1)

            def pre1():
                repeat(1, s1_bank(3), ((bk_rep[1], bk_col[1]), (bv1_rep, bv1_col)))
                dve.wait_ge(rows_loaded, 16 * 2)
                for h in range(2):
                    dve.wait_ge(out_free[h], 16)
                nc.vector.tensor_tensor(betaob_part, beta_row, bo_row, ALU.add).then_inc(row1_made, 1)
                dve.wait_ge(made_sb, 4)
                for c in range(EC):
                    nc.vector.tensor_scalar(a1_gamma[:, c, :], a1_sb[:, c, :], gamma_col[:, c:c + 1], SCALE, ALU.mult, ALU.mult
                                            ).then_inc(row1_made, 1)
                nc.vector.scalar_tensor_tensor(u1_gamma[:], u1_row, SCALE, gamma_row[:], ALU.mult, ALU.mult
                                               ).then_inc(row1_made, 1)
                dve.wait_ge(wv0_hi_done, 1)
                weight_low(wv0_lo[:], wv0_sb, wv0_hi[:])
                dve.wait_ge(made_sb, 5)
                dve.wait_ge(row1_made, 1)
                nc.vector.tensor_tensor(betaob_row[:], s1_bank(3)[:, E:2 * E], betaob_part, ALU.add).then_inc(row1_made, 1)
                dve.wait_ge(small_sb, 2)
                nc.vector.tensor_scalar(scaled1[:], small[1][:], SCALE, None, ALU.mult).then_inc(row1_made, 1)
                dve.wait_ge(row1_made, MADE - 1)
                nc.vector.tensor_tensor_reduce(out=xr[:, 0, :], in0=u1_row, in1=beta_row, scale=SCALE,
                                               scalar=scaled1[:, 1:2], op0=ALU.mult, op1=ALU.add,
                                               accum_out=c1_const[:, 0:1]).then_inc(row1_made, 1)

            steps = {f.__name__: f for f in (
                ctxT_low, xT_low, at0_low, bias_x0, q0_low, max0, recip0, p0_low, residual0, moments0, normalised, bias_row1, q1_low, rowmax1, bias1_of, recip1, p1_low, finish)}

            def body(a, b, c, done=()):
                for name, who, i in VECTOR_ORDER:
                    bt = {"a": a, "b": b, "c": c}[who]
                    if bt and (name, i) not in done:
                        steps[name](bt, i)

            run(body, (pre0, pre1), dve)

        @blk.gpsimd
        def _(pool):
            def ctx_low(a, g):
                pool.wait_ge(ctx_hi_done, GROUPS * a.n + g + 1)
                m = rows(group(g)[0])
                tiles = slice(group(g)[0], group(g)[-1] + 1)
                nc.gpsimd.tensor_tensor(ctx_lo[a.par][0:m, tiles, :], ctx_sb[0:m, tiles, :],
                                        ctx_hi[a.par][0:m, tiles, :].bitcast(F32), ALU.subtract).then_inc(ctx_lo_done, 1)

            def sum_weights(a, i):
                pool.wait_ge(p0_lo_done, MT * a.n + i + 1)
                m = rows(i)
                total = wsum[a.par][0:m, :]
                hi, lo = (part[0:m, ring0(i), :].bitcast(F32) for part in (p0_hi, p0_lo))
                if i == 0:
                    nc.gpsimd.tensor_tensor(total, hi, lo, ALU.add).then_inc(wsum_done, 1)
                else:
                    pool.wait_ge(wsum_done, MT * a.n + i)
                    nc.gpsimd.tensor_tensor(total, total, lo, ALU.add).then_inc(wsum_part, 1)
                    pool.wait_ge(wsum_part, (MT - 1) * a.n + i)
                    nc.gpsimd.tensor_tensor(total, total, hi, ALU.add).then_inc(wsum_done, 1)

            def residual1(b, _):
                pool.wait_ge(row1_made, MADE)
                pool.wait_ge(xhat_done, TB * (b.n + 1))
                for h in range(2):
                    pool.wait_ge(out_free[h], 16 * (b.n + 1))
                for t in range(TB):
                    ins = nc.gpsimd.tensor_tensor(y_res[:, t, :], xhat[:, t, :], gamma_row[:], ALU.mult)
                ins.then_inc(y_part_done, 1)
                pool.wait_ge(y_part_done, b.n + 1)
                for t in range(TB):
                    ins = nc.gpsimd.tensor_tensor(y_res[:, t, :], y_res[:, t, :], betaob_row[:], ALU.add)
                ins.then_inc(y_res_done, 1)

            def rsqrt_var(a, h):
                pool.wait_ge(var_done, 2 * a.n + h + 1)
                two = slice(2 * h, 2 * h + 2)
                nc.gpsimd.tensor_tensor(rstd[:, two, :], var_eps[:, two, :], neg_half[:], ALU.pow).then_inc(rstd_done, 1)

            def pre0():
                nc.gpsimd.memset(neg_half[:], -0.5)
                nc.gpsimd.memset(ident[:], 0.0).then_inc(ident_zero, 1)
                pool.wait_ge(ident_zero, 1)
                nc.gpsimd.affine_select(out=ident[:], in_=ident[:], compare_op=ALU.not_equal, fill=1.0, base=0,
                                        pattern=[[-1, P]], channel_multiplier=1).then_inc(ident_done, 1)

            def pre1():
                pass

            steps = {f.__name__: f for f in (
                ctx_low, sum_weights, rsqrt_var, residual1)}

            def body(a, b, c, done=()):
                for name, who, i in GPSIMD_ORDER:
                    bt = {"a": a, "b": b, "c": c}[who]
                    if bt and (name, i) not in done:
                        steps[name](bt, i)

            run(body, (pre0, pre1), pool)


_INS = ["x", "ctx_512"] + [f"L0_xattn_{n}" for n in ("Wq", "bq", "Wk", "bk", "Wv", "bv", "gamma", "beta")] + [
    f"L1_xattn_{n}" for n in ("Wq", "bq", "Wk", "bk", "Wv", "bv", "Wo", "bo")]


def kernel(**inputs):
    import numpy as np
    import concourse.bacc as bacc
    from concourse.bass_utils import run_bass_kernel_spmd

    nc = bacc.Bacc("TRN2", target_bir_lowering=False, num_devices=1)
    arrays, args = {}, []
    for name in _INS:
        a = np.ascontiguousarray(inputs[name])
        arrays[f"in_{name}_dram"] = a
        args.append(nc.dram_tensor(f"in_{name}_dram", a.shape, mybir.dt.from_np(a.dtype), kind="ExternalInput").ap())
    shape = inputs["x"].shape
    args.append(nc.dram_tensor("out_dram", shape, F32, kind="ExternalOutput").ap())
    xattn_kernel(nc, *args)
    r = run_bass_kernel_spmd(nc, [arrays], core_ids=[0])
    return r.results[0]["out_dram"]
```
